# Optimizing a Trainium2 kernel written in Bass

```python
import numpy as np
import jax
import jax.numpy as jnp

def _softmax(x, axis=-1):
    return jax.nn.softmax(x, axis=axis)

def _gelu(x):
    return jax.nn.gelu(x, approximate=True)

def _silu(x):
    return jax.nn.silu(x)

def _sigmoid(x):
    return jax.nn.sigmoid(x)

def _layernorm(x, axis=-1, eps=1e-05):
    m = jnp.mean(x, axis=axis, keepdims=True)
    v = jnp.var(x, axis=axis, keepdims=True)
    return (x - m) / jnp.sqrt(v + eps)

def _scatter_add(tgt, idx, src, axis=0):
    return tgt.at[idx].add(src)

def _segment_sum(src, seg, n):
    return jax.ops.segment_sum(src, seg, n)
kernel_name = 'mk_adj_seq_d2_adj_r2_c8966f'

def setup_inputs(seed: int=0):
    np.random.seed(seed)
    _w = jnp.asarray

    def _rec_inputs():
        import jax
        import jax.numpy as jnp
        _gk = jax.random.key(seed)
        x = -0.0005207 + 1.001 * jax.random.normal(jax.random.fold_in(_gk, 1), (16, 512, 256), jnp.float32)
        _w = (1.0 + jnp.arange(512, dtype=jnp.float32)) ** (-0.5)
        _w = _w / _w.mean()
        _pij = jnp.clip(0.00390625 * _w[:, None] * _w[None, :], 0.0, 1.0)
        _a = jax.random.uniform(jax.random.fold_in(_gk, 2), (16, 512, 512)) < _pij
        _a = jnp.logical_or(_a, jnp.swapaxes(_a, -1, -2))
        _a = jnp.logical_or(_a, jnp.eye(512, dtype=bool))
        _af = _a.astype(jnp.float32)
        _af = _af * jax.random.uniform(jax.random.fold_in(_gk, 3), (16, 512, 512), jnp.float32, 0.05, 5.22011)
        adj = _af
        return (x, adj)
    x, adj = _rec_inputs()

    def _L0_gnn_setup():
        import jax, jax.numpy as jnp
        import numpy as np
        EPS = 1e-06
        ALPHA = 0.2

        def layer_norm(x, g, b):
            mu = jnp.mean(x, axis=-1, keepdims=True)
            var = jnp.mean(jnp.square(x - mu), axis=-1, keepdims=True)
            return (x - mu) * jax.lax.rsqrt(var + EPS) * g + b

        def graph_attention(x, bias, W, a_src, a_dst):
            B, N, D = x.shape
            H, Dh = a_src.shape
            h = jnp.einsum('bnd,dhk->bhnk', x, W.reshape(D, H, Dh))
            s = jnp.einsum('bhnk,hk->bhn', h, a_src)
            t = jnp.einsum('bhnk,hk->bhn', h, a_dst)
            e = jax.nn.leaky_relu(s[:, :, :, None] + t[:, :, None, :], ALPHA)
            e = e + bias[:, None, :, :]
            attn = jax.nn.softmax(e, axis=-1)
            out = jnp.einsum('bhij,bhjk->bhik', attn, h)
            return out.transpose(0, 2, 1, 3).reshape(B, N, H * Dh)
        key = jax.random.key(seed)
        ks = jax.random.split(key, 8)
        B, N, D, H = (2, 1024, 256, 8)
        Dh = D // H
        sc = 1.0 / np.sqrt(D)
        return {'x': jax.random.normal(ks[0], (B, N, D), jnp.float32), 'bias': jax.random.normal(ks[1], (B, N, N), jnp.float32), 'W1': jax.random.normal(ks[2], (D, D), jnp.float32) * sc, 'a_src1': jax.random.normal(ks[3], (H, Dh), jnp.float32) * sc, 'a_dst1': jax.random.normal(ks[4], (H, Dh), jnp.float32) * sc, 'g1': jnp.ones((D,), jnp.float32), 'b1': jnp.zeros((D,), jnp.float32), 'W2': jax.random.normal(ks[5], (D, D), jnp.float32) * sc, 'a_src2': jax.random.normal(ks[6], (1, D), jnp.float32) * sc, 'a_dst2': jax.random.normal(ks[7], (1, D), jnp.float32) * sc, 'g2': jnp.ones((D,), jnp.float32), 'b2': jnp.zeros((D,), jnp.float32)}
    _L0_gnn_all = _L0_gnn_setup()
    _L0_gnn_in = {k: v for k, v in _L0_gnn_all.items() if k in ('W1', 'a_src1', 'a_dst1', 'g1', 'b1', 'W2', 'a_src2', 'a_dst2', 'g2', 'b2')}
    del _L0_gnn_all

    def _L1_gnn_setup():
        import jax, jax.numpy as jnp
        import numpy as np
        NUM_HEADS = 8
        EPS = 1e-09
        key = jax.random.key(seed)
        ks = jax.random.split(key, 8)
        B, N, D = (2, 1024, 256)
        s = 1.0 / np.sqrt(D)
        x = jax.random.normal(ks[0], (B, N, D), dtype=jnp.float32)
        adjacency = jax.random.uniform(ks[1], (B, N, N), dtype=jnp.float32)
        W_q = jax.random.normal(ks[2], (D, D), dtype=jnp.float32) * s
        W_k = jax.random.normal(ks[3], (D, D), dtype=jnp.float32) * s
        W_v = jax.random.normal(ks[4], (D, D), dtype=jnp.float32) * s
        b_q = jnp.zeros((D,), jnp.float32)
        b_k = jnp.zeros((D,), jnp.float32)
        b_v = jnp.zeros((D,), jnp.float32)
        w_g = jax.random.normal(ks[5], (2 * D,), dtype=jnp.float32) * (1.0 / np.sqrt(2 * D))
        b_g = jnp.zeros((), jnp.float32)
        return {'x': x, 'adjacency': adjacency, 'W_q': W_q, 'b_q': b_q, 'W_k': W_k, 'b_k': b_k, 'W_v': W_v, 'b_v': b_v, 'w_g': w_g, 'b_g': b_g}
    _L1_gnn_all = _L1_gnn_setup()
    _L1_gnn_in = {k: v for k, v in _L1_gnn_all.items() if k in ('W_q', 'b_q', 'W_k', 'b_k', 'W_v', 'b_v', 'w_g', 'b_g')}
    del _L1_gnn_all
    return {'x': x, 'adj': adj, 'L0_gnn_W1': _L0_gnn_in['W1'], 'L0_gnn_a_src1': _L0_gnn_in['a_src1'], 'L0_gnn_a_dst1': _L0_gnn_in['a_dst1'], 'L0_gnn_g1': _L0_gnn_in['g1'], 'L0_gnn_b1': _L0_gnn_in['b1'], 'L0_gnn_W2': _L0_gnn_in['W2'], 'L0_gnn_a_src2': _L0_gnn_in['a_src2'], 'L0_gnn_a_dst2': _L0_gnn_in['a_dst2'], 'L0_gnn_g2': _L0_gnn_in['g2'], 'L0_gnn_b2': _L0_gnn_in['b2'], 'L1_gnn_W_q': _L1_gnn_in['W_q'], 'L1_gnn_b_q': _L1_gnn_in['b_q'], 'L1_gnn_W_k': _L1_gnn_in['W_k'], 'L1_gnn_b_k': _L1_gnn_in['b_k'], 'L1_gnn_W_v': _L1_gnn_in['W_v'], 'L1_gnn_b_v': _L1_gnn_in['b_v'], 'L1_gnn_w_g': _L1_gnn_in['w_g'], 'L1_gnn_b_g': _L1_gnn_in['b_g']}

def reference(x, adj, L0_gnn_W1, L0_gnn_a_src1, L0_gnn_a_dst1, L0_gnn_g1, L0_gnn_b1, L0_gnn_W2, L0_gnn_a_src2, L0_gnn_a_dst2, L0_gnn_g2, L0_gnn_b2, L1_gnn_W_q, L1_gnn_b_q, L1_gnn_W_k, L1_gnn_b_k, L1_gnn_W_v, L1_gnn_b_v, L1_gnn_w_g, L1_gnn_b_g):
    import jax
    import jax.numpy as jnp

    def _L0_gnn_ref(x, bias, W1, a_src1, a_dst1, g1, b1, W2, a_src2, a_dst2, g2, b2):
        import jax, jax.numpy as jnp
        import numpy as np
        EPS = 1e-06
        ALPHA = 0.2

        def layer_norm(x, g, b):
            mu = jnp.mean(x, axis=-1, keepdims=True)
            var = jnp.mean(jnp.square(x - mu), axis=-1, keepdims=True)
            return (x - mu) * jax.lax.rsqrt(var + EPS) * g + b

        def graph_attention(x, bias, W, a_src, a_dst):
            B, N, D = x.shape
            H, Dh = a_src.shape
            h = jnp.einsum('bnd,dhk->bhnk', x, W.reshape(D, H, Dh))
            s = jnp.einsum('bhnk,hk->bhn', h, a_src)
            t = jnp.einsum('bhnk,hk->bhn', h, a_dst)
            e = jax.nn.leaky_relu(s[:, :, :, None] + t[:, :, None, :], ALPHA)
            e = e + bias[:, None, :, :]
            attn = jax.nn.softmax(e, axis=-1)
            out = jnp.einsum('bhij,bhjk->bhik', attn, h)
            return out.transpose(0, 2, 1, 3).reshape(B, N, H * Dh)
        attn_in = layer_norm(x, g1, b1)
        attn = graph_attention(attn_in, bias, W1, a_src1, a_dst1) + x
        attn_in2 = layer_norm(attn, g2, b2)
        out = graph_attention(attn_in2, bias, W2, a_src2, a_dst2) + attn
        return out

    def _L1_gnn_ref(x, adjacency, W_q, b_q, W_k, b_k, W_v, b_v, w_g, b_g):
        import jax, jax.numpy as jnp
        import numpy as np
        NUM_HEADS = 8
        EPS = 1e-09
        B, N, D = x.shape
        H = NUM_HEADS
        hd = D // H
        Q = (x @ W_q + b_q).reshape(B, N, H, hd)
        K = (x @ W_k + b_k).reshape(B, N, H, hd)
        V = (x @ W_v + b_v).reshape(B, N, H, hd)
        scores = jnp.einsum('bihd,bjhd->bhij', Q, K) / jnp.sqrt(jnp.float32(hd))
        a = x @ w_g[:D]
        c = x @ w_g[D:]
        soul_bias = a[:, :, None] + c[:, None, :] + b_g
        scores = scores + (soul_bias + jnp.log(adjacency + EPS))[:, None, :, :]
        attn = jax.nn.softmax(scores, axis=-1)
        out = jnp.einsum('bhij,bjhd->bihd', attn, V).reshape(B, N, D)
        return out + x
    x = _L0_gnn_ref(x, adj, L0_gnn_W1, L0_gnn_a_src1, L0_gnn_a_dst1, L0_gnn_g1, L0_gnn_b1, L0_gnn_W2, L0_gnn_a_src2, L0_gnn_a_dst2, L0_gnn_g2, L0_gnn_b2)
    x = _L1_gnn_ref(x, adj, L1_gnn_W_q, L1_gnn_b_q, L1_gnn_W_k, L1_gnn_b_k, L1_gnn_W_v, L1_gnn_b_v, L1_gnn_w_g, L1_gnn_b_g)
    return x

_drawn_inputs = setup_inputs


def setup_inputs(seed=0):
    import zlib

    import numpy as np

    out = dict(_drawn_inputs(seed))
    spreads = {'L0_gnn_g1': (1.0, 0.2),
     'L0_gnn_b1': (0.0, 0.1),
     'L0_gnn_g2': (1.0, 0.2),
     'L0_gnn_b2': (0.0, 0.1),
     'L1_gnn_b_q': (0.0, 0.296),
     'L1_gnn_b_k': (0.0, 0.8),
     'L1_gnn_b_v': (0.0, 0.1)}
    factors = {}
    for name, (base, spread) in spreads.items():
        noise = np.random.default_rng([zlib.crc32(name.encode()), seed]).standard_normal(out[name].shape)
        drawn = base * np.exp(spread * noise) if base else spread * noise
        out[name] = jnp.asarray(drawn.astype(out[name].dtype))
    for name, factor in factors.items():
        out[name] = (out[name] * factor).astype(out[name].dtype)
    return out
```

```python
from contextlib import ExitStack

import concourse.bass as bass
from concourse import mybir

F32 = mybir.dt.float32
F32R = mybir.dt.float32r
ALU = mybir.AluOpType
ACT = mybir.ActivationFunctionType
AX_X = mybir.AxisListType.X

P = 128


class Banks:

    def __init__(self, uses, slots, filled, emptied):
        self.uses, self.slots, self.filled, self.emptied = uses, slots, filled, emptied
        self.at = {key: n for n, (key, _) in enumerate(uses)}
        self.per_batch = len(uses)
        self.total = {r: sum(engine == r for _, engine in uses) for r in emptied}

    def slot(self, key):
        return self.at[key] % self.slots

    def wait_free(self, pe, b, key):
        n = self.at[key] - self.slots
        if n < 0:
            for r, s in self.emptied.items():
                pe.wait_ge(s, b * self.total[r])
            return
        r = self.uses[n][1]
        pe.wait_ge(self.emptied[r], b * self.total[r] + sum(engine == r for _, engine in self.uses[:n + 1]))

    def count_filled(self, b, key):
        return b * self.per_batch + self.at[key] + 1

    def count_emptied(self, b, key):
        n = self.at[key]
        r = self.uses[n][1]
        return b * self.total[r] + sum(engine == r for _, engine in self.uses[:n + 1])

    def wait_filled(self, eng, b, key):
        eng.wait_ge(self.filled, self.count_filled(b, key))

    def wait_emptied(self, eng, b, key):
        eng.wait_ge(self.emptied[self.uses[self.at[key]][1]], self.count_emptied(b, key))


def two_gat_layers_then_biased_attention(
    nc, x, adj, W1, a_src1, a_dst1, g1, b1, W2, a_src2, a_dst2, g2, b2,
    W_q, b_q, W_k, b_k, W_v, b_v, w_g, b_g, out,
):
    B, N, D = x.shape
    H, DH = a_src1.shape
    IT = N // P
    KT = D // P
    QUADS = H // 4
    SCALE = float(DH) ** -0.5
    LN_EPS = 1e-6
    ADJ_EPS = 1e-9
    SLOPE = 0.2
    PBUFS = 3
    assert DH == 32 and D == 256 and N == 512 and KT == QUADS == 2

    p_uses = [("gat1", q, jt) for q in range(QUADS) for jt in range(IT)] + [("gat2", 0, 0)] \
        + [("att", q, jt) for q in range(QUADS) for jt in range(IT)]
    NPU = len(p_uses)
    pool_uses = [u for n, u in enumerate(p_uses) if u[0] == "att" and n % 3 == 1]
    dve_uses = [u for u in p_uses if u not in pool_uses]

    with ExitStack() as ctx:
        def sb(name, shape, dt=F32):
            return ctx.enter_context(nc.sbuf_tensor(name, shape, dt))

        def sem(name):
            return ctx.enter_context(nc.semaphore(name))

        ident = sb("ident", [P, P])
        select_head = sb("select_head", [P, H, P], F32R)
        ones = sb("ones", [P, DH])
        minus_half = sb("minus_half", [P, IT])
        w1 = sb("w1", [P, KT, D])
        w2 = sb("w2", [P, KT, D])
        wq = sb("wq", [P, KT, D])
        wk = sb("wk", [P, KT, D])
        wv = sb("wv", [P, KT, D])
        wg = sb("wg", [P, KT, 64])
        wa1 = sb("wa1", [P, KT, 64])
        wa2 = sb("wa2", [P, KT, 64])
        gb = sb("gb", [P, 4, KT])
        qk_bias = sb("qk_bias", [P, 3, KT])
        bv = sb("bv", [P, D])
        bg = sb("bg", [64, 1])

        x_rows = sb("x_rows", [P, IT, D])
        adj_rows = sb("adj_rows", [P, IT, N])
        neg_adj_max = sb("neg_adj_max", [P, IT])
        exp_adj = sb("exp_adj", [P, IT, N])
        exp_adj_t = sb("exp_adj_t", [P, IT, N])
        adj_t = sb("adj_t", [P, IT, N])
        stats = sb("stats", [P, IT, 6])
        mean_var = sb("mean_var", [P, IT, 2])
        var_eps = sb("var_eps", [P, 2, IT])
        rstd = sb("rstd", [P, 2, IT])
        normed = sb("normed", [P, IT, D])
        feat_t = sb("feat_t", [P, 2, KT, N])
        s_row = sb("s_row", [H, N])
        t_row = sb("t_row", [H, N])
        z_row = sb("z_row", [H, N])
        t_max = sb("t_max", [H, 2, 2])
        g_row = sb("g_row", [H, N])
        g_hl = sb("g_hl", [P, N], F32R)
        c_rows = sb("c_rows", [P, N])
        c_cols = sb("c_cols", [P, 2, IT, 64])
        g_all = sb("g_all", [P, H, N])
        g_one = sb("g_one", [P, N])
        v1 = sb("v1", [P, IT, H, DH])
        d1 = sb("d1", [P, IT, H, DH])
        v2 = sb("v2", [P, IT, D + 4])
        v3 = v1[:].rearrange("p t h d -> p t (h d)")
        probs = sb("probs", [P, PBUFS, 4, N])
        select_f32 = probs[:, 0, 0:2, :].rearrange("p a (c n) -> p (a c) n", n=P)
        a_rows = probs[:, 0, 2:4, :].rearrange("p a (c n) -> p (a c) n", n=D)
        minus_head_f32 = probs[0:H, 1, 0:2, :].rearrange("p a (c n) -> p (a c) n", n=P)
        minus_head = probs[0:H, 1, 2:4, :].rearrange("p a (c n) -> p (a c) n", n=P).bitcast(F32R)
        ones_f32 = probs[0:2, 2, 0, :]
        ones_r = probs[0:2, 2, 1, :].bitcast(F32R)
        wa_tmp = probs[:, 2, 2, 0:D]
        recip = sb("recip", [P, N])
        spare = sb("spare", [P, 1])
        recip1 = sb("recip1", [P, IT])
        heads_t = sb("heads_t", [P, 2, QUADS, N])
        x2 = sb("x2", [P, IT, D])
        x3 = sb("x3", [P, IT, D])
        q_f32, k_f32 = exp_adj[:, 0:2, :], exp_adj[:, 2:4, :]
        q_hi = sb("q_hi", [P, KT, N], F32R)
        q_lo = sb("q_lo", [P, KT, N], F32R)
        k_hi = sb("k_hi", [P, KT, N], F32R)
        k_lo = sb("k_lo", [P, KT, N], F32R)
        ac_f32 = sb("ac_f32", [64, N])
        ac_hi = sb("ac_hi", [64, N], F32R)
        ac_lo = sb("ac_lo", [64, N], F32R)
        row_max = sb("row_max", [P, IT, H])
        max_t = sb("max_t", [H, N], F32R)
        q_stack = sb("q_stack", [P, H, N], F32R)
        k_stack = sb("k_stack", [P, H, N], F32R)
        out_rows = normed

        pair = ctx.enter_context(nc.psum_tensor("pair", [P, 2, 2, N], F32))
        heads_ps = ctx.enter_context(nc.psum_tensor("heads_ps", [P, 2, N], F32))
        work = ctx.enter_context(nc.psum_tensor("work", [P, 2, N], F32))

        weights_loaded = sem("weights_loaded")
        consts_made = sem("consts_made")
        rounded_consts = sem("rounded_consts")
        rounded_selector = sem("rounded_selector")
        vec_cleared = sem("vec_cleared")
        wa_products = sem("wa_products")
        rows_filled = sem("rows_filled")
        stack_consts = sem("stack_consts")
        wa_ready = sem("wa_ready")
        vec_setup = sem("vec_setup")
        x_loaded = sem("x_loaded")
        adj_loaded = sem("adj_loaded")
        adj_max_ready = sem("adj_max_ready")
        exp_adj_ready = sem("exp_adj_ready")
        var_ready = sem("var_ready")
        rstd_ready = sem("rstd_ready")
        normed_ready = sem("normed_ready")
        st_rows_ready = sem("st_rows_ready")
        exp_rows_ready = sem("exp_rows_ready")
        g_split = sem("g_split")
        qk_split = sem("qk_split")
        stacks_loaded = sem("stacks_loaded")
        max_loaded = sem("max_loaded")
        probs_dve = sem("probs_dve")
        probs_pool = sem("probs_pool")
        probs_used = sem("probs_used")
        heads_emptied = sem("heads_emptied")
        stored = sem("stored")
        vec_step = sem("vec_step")

        work_ring = Banks(
            [(("adj_t", jt), "act") for jt in range(IT)] + [(("exp_t", jt), "act") for jt in range(IT)]
            + [(("feat", 0, m), "act") for m in range(KT)] + [(("st", 0), "dve"), (("cols", 0), "act")]
            + [(("feat", 1, m), "act") for m in range(KT)] + [(("st", 1), "dve"), (("cols", 1), "act")]
            + [(("feat", 2, m), "act") for m in range(KT)]
            + [(("q", m), "act") for m in range(KT)] + [(("k", m), "act") for m in range(KT)]
            + [(("ac",), "act"), (("max_t",), "act")],
            2, sem("work_filled"), {"act": sem("work_emptied_act"), "dve": sem("work_emptied_dve")})
        pair_ring = Banks(
            [(("h", 0), "dve")] + [(("g", n), "act") for n in range(H // 2)] + [(("back", 0), "dve")]
            + [(("h", 1), "dve"), (("g2",), "act"), (("v",), "dve")]
            + [(("max", h, ip), "dve") for h in range(H) for ip in range(IT // 2)]
            + [(("score", q, jt, hp), "act") for q in range(QUADS) for jt in range(IT) for hp in range(2)]
            + [(("back", 1), "dve")],
            2, sem("pair_filled"), {"act": sem("pair_emptied_act"), "dve": sem("pair_emptied_dve")})
        act_work, dve_work = work_ring.emptied["act"], work_ring.emptied["dve"]
        act_pair, dve_pair = pair_ring.emptied["act"], pair_ring.emptied["dve"]

        def work_bank(key):
            return work[:, work_ring.slot(key), :]

        def pair_banks(key):
            return pair[:, pair_ring.slot(key), :, :]

        def pair_rows(key):
            return pair_banks(key).rearrange("p a (c d) -> p (a c) d", d=D)

        def by_feature(w):
            return w.rearrange("(k p) n -> p k n", p=P)

        def column(v):
            return v.rearrange("(k p) -> p k", p=P)

        weight_loads = [(w1[:], by_feature(W1)), (w2[:], by_feature(W2)), (wq[:], by_feature(W_q)),
                        (wk[:], by_feature(W_k)), (wv[:], by_feature(W_v))]
        weight_loads += [(gb[:, n, :], column(v)) for n, v in enumerate((g1, b1, g2, b2))]
        weight_loads += [(qk_bias[:, n, :], column(v)) for n, v in enumerate((b_q, b_k))]
        weight_loads += [(a_rows[:, n, :], v.rearrange("h d -> (h d)").partition_broadcast(P))
                         for n, v in enumerate((a_src1, a_dst1, a_src2, a_dst2))]
        weight_loads += [(bv[:], b_v.partition_broadcast(P))]
        gate_loads = [(bg[0:1, :], b_g.rearrange("(a b) -> a b", a=1))]
        gate = w_g.rearrange("(s k p) -> p s k", p=P, k=KT)
        gate_loads += [(wg[:, k, 32 * s:32 * s + 1], gate[:, s, k:k + 1]) for s in range(2) for k in range(KT)]
        N_WEIGHT_LOADS = len(weight_loads) + len(gate_loads)
        CONSTS = 15

        STACK_DMAS = 4 * 6 + 4
        VEC_STEPS = 16
        HEAD_USES = QUADS + IT + QUADS

        x_tiles = x.rearrange("b (t p) d -> b p t d", p=P)
        adj_tiles = adj.rearrange("b (t p) n -> b p t n", p=P)
        out_tiles = out.rearrange("b (t p) d -> b p t d", p=P)

        def use(u):
            return p_uses.index(u)

        def wait_probs_free(eng, b, u):
            n = use(u) - PBUFS
            eng.wait_ge(probs_used, b * NPU + max(n + 1, 0))

        block = ctx.enter_context(nc.Block())

        @block.sync
        def _(sp):
            q_raw, k_raw = q_stack[:].bitcast(F32), k_stack[:].bitcast(F32)
            for dst, src in weight_loads:
                sp.dma_start(dst, src, allow_slow_non_contiguous=True).then_inc(weights_loaded, 16)
            sp.wait_ge(consts_made, CONSTS)
            for dst, src in gate_loads:
                sp.dma_start(dst, src, allow_slow_non_contiguous=True).then_inc(weights_loaded, 16)
            sp.wait_ge(rounded_consts, 2)
            sp.dma_start(k_raw[96:98, :, :], ones_r.bitcast(F32).unsqueeze(1).broadcast_to((2, H, N))).then_inc(stack_consts, 16)
            sp.dma_start(q_raw[98:100, :, :], ones_r.bitcast(F32).unsqueeze(1).broadcast_to((2, H, N))).then_inc(stack_consts, 16)
            for n in range(N // P):
                sp.dma_start(k_raw[104:104 + H, :, n * P:(n + 1) * P], minus_head.bitcast(F32)).then_inc(stack_consts, 16)

            def load(b):
                sp.dma_start(adj_rows[:], adj_tiles[b]).then_inc(adj_loaded, 16)
                sp.dma_start(x_rows[:], x_tiles[b]).then_inc(x_loaded, 16)

            def batch(b, last):
                sp.wait_ge(qk_split, b + 1)
                pair_ring.wait_filled(sp, b, ("h", 1))
                for rows, parts in ((q_raw, (q_hi, q_hi, q_lo)), (k_raw, (k_hi, k_lo, k_hi))):
                    for n, part in enumerate(parts):
                        for g in range(4):
                            sp.dma_start(rows[32 * n:32 * n + 32, g:H:4, :],
                                         part[32 * g:32 * g + 32, :, :].bitcast(F32)).then_inc(stacks_loaded, 16)
                for n, (rows, part, r) in enumerate(((q_raw, ac_hi, 0), (q_raw, ac_lo, 0),
                                                     (k_raw, ac_hi, 32), (k_raw, ac_lo, 32))):
                    sp.dma_start(rows[96 + n:97 + n, :, :],
                                 part[r:r + 1, :].bitcast(F32).unsqueeze(1).broadcast_to((1, H, N))
                                 ).then_inc(stacks_loaded, 16)
                if not last:
                    work_ring.wait_filled(sp, b, ("adj_t", IT - 1))
                    sp.wait_ge(exp_adj_ready, b * IT + IT)
                    sp.wait_ge(var_ready, b * 2 + 2)
                    load(b + 1)
                work_ring.wait_emptied(sp, b, ("max_t",))
                sp.dma_start(q_raw[104:104 + H, :, :],
                             max_t[:].bitcast(F32).unsqueeze(1).broadcast_to((H, H, N))).then_inc(max_loaded, 16)
                pair_ring.wait_emptied(sp, b, ("back", 1))
                sp.dma_start(out_tiles[b], out_rows[:]).then_inc(stored, 16)

            load(0)
            with sp.Fori(0, B - 1) as b:
                batch(b, False)
            batch(B - 1, True)
            sp.wait_ge(stored, 16 * B)

        @block.gpsimd
        def _(pool):
            pool.memset(ident[:], 0.0).then_inc(consts_made, 1)
            pool.memset(select_f32, 0.0).then_inc(consts_made, 1)
            pool.memset(minus_head_f32, 0.0).then_inc(consts_made, 1)
            pool.memset(ones_f32, 1.0).then_inc(consts_made, 1)
            pool.memset(ones[:], 1.0).then_inc(consts_made, 1)
            pool.memset(minus_half[:], -0.5).then_inc(consts_made, 1)
            pool.memset(wg[:], 0.0).then_inc(consts_made, 1)
            pool.memset(bg[:], 0.0).then_inc(consts_made, 1)
            pool.wait_ge(consts_made, 8)
            pool.affine_select(out=ident[:], in_=ident[:], compare_op=ALU.not_equal, fill=1.0, base=0,
                               pattern=[[-1, P]], channel_multiplier=1).then_inc(consts_made, 1)
            pool.affine_select(out=select_f32, in_=select_f32, compare_op=ALU.not_equal, fill=1.0, base=0,
                               pattern=[[-1, H], [0, P]], channel_multiplier=1).then_inc(consts_made, 1)
            pool.affine_select(out=minus_head_f32, in_=minus_head_f32, compare_op=ALU.not_equal, fill=-1.0,
                               base=0, pattern=[[-1, H], [0, P]], channel_multiplier=1).then_inc(consts_made, 1)
            pool.wait_ge(consts_made, 11)
            pool.affine_select(out=select_f32, in_=select_f32, compare_op=ALU.not_equal, fill=1.0, base=-32,
                               pattern=[[-1, H], [0, P]], channel_multiplier=1).then_inc(consts_made, 1)
            pool.memset(c_rows[:], 0.0).then_inc(consts_made, 1)
            for n, rows in enumerate((q_stack, k_stack)):
                pool.wait_ge(consts_made, 13 + n)
                pool.memset(rows[96:P, :, :].bitcast(F32), 0.0).then_inc(consts_made, 1)

            pool.wait_ge(consts_made, CONSTS)
            with pool.Fori(0, B) as b:
                for layer in range(2):
                    pool.wait_ge(var_ready, b * 2 + layer + 1)
                    pool.tensor_tensor(rstd[:, layer, :], var_eps[:, layer, :], minus_half[:],
                                       ALU.pow).then_inc(rstd_ready, 1)
                for u in pool_uses:
                    _, q, jt = u
                    pair_ring.wait_emptied(pool, b, ("score", q, jt, 1))
                    p = probs[:, use(u) % PBUFS, :, :]
                    pool.tensor_tensor(p, p, adj_t[:, jt:jt + 1, :].broadcast_to((P, 4, N)),
                                       ALU.mult).then_inc(probs_pool, 1)

        @block.scalar
        def _(act):
            act.wait_ge(weights_loaded, 16 * N_WEIGHT_LOADS)
            act.mul(qk_bias[:, 2, :], qk_bias[:, 0, :], SCALE).then_inc(vec_setup, 1)
            act.wait_ge(vec_setup, 1)

            def turn_features(b, layer):
                for m in range(KT):
                    key = ("feat", layer, m)
                    work_ring.wait_filled(act, b, key)
                    if layer < 2:
                        nc.scalar.activation(feat_t[:, layer % 2, m, :], work_bank(key), ACT.Identity,
                                             bias=gb[:, 2 * layer + 1, m:m + 1],
                                             scale=gb[:, 2 * layer, m:m + 1]).then_inc(act_work, 1)
                    else:
                        nc.scalar.activation(feat_t[:, layer % 2, m, :], work_bank(key),
                                             ACT.Copy).then_inc(act_work, 1)

            def gat_factors(b, layer):
                heads = H if layer == 0 else 1
                act.wait_ge(st_rows_ready, b * 2 + layer + 1)
                nc.scalar.activation(c_rows[0:heads, :], z_row[0:heads, :], ACT.Exp)
                nc.scalar.activation(c_rows[32:32 + heads, :], z_row[0:heads, :], ACT.Exp,
                                     scale=-(1.0 - SLOPE))
                nc.scalar.activation(g_row[0:heads, :], s_row[0:heads, :], ACT.Exp,
                                     bias=t_max[0:heads, layer, 1:2], scale=1.0 - SLOPE).then_inc(exp_rows_ready, 1)
                key = ("cols", layer)
                work_ring.wait_filled(act, b, key)
                nc.scalar.activation(c_cols[:, layer, :, :],
                                     work_bank(key).rearrange("p (t c) -> p t c", c=P)[:, :, 0:64],
                                     ACT.Copy).then_inc(act_work, 1)

            with act.Fori(0, B) as b:
                act.wait_ge(adj_loaded, b * 16 + 16)
                act.wait_ge(adj_max_ready, b + 1)
                act.wait_ge(qk_split, b)
                act.wait_ge(work_ring.filled, b * work_ring.per_batch)
                for it in range(IT):
                    nc.scalar.activation(exp_adj[:, it, :], adj_rows[:, it, :], ACT.Exp,
                                         bias=neg_adj_max[:, it:it + 1]).then_inc(exp_adj_ready, 1)
                act.wait_ge(probs_dve, b * len(dve_uses))
                act.wait_ge(probs_pool, b * len(pool_uses))
                for jt in range(IT):
                    work_ring.wait_filled(act, b, ("adj_t", jt))
                    nc.scalar.activation(adj_t[:, jt, :], work_bank(("adj_t", jt)), ACT.Copy,
                                         bias=ADJ_EPS).then_inc(act_work, 1)
                for jt in range(IT):
                    work_ring.wait_filled(act, b, ("exp_t", jt))
                    nc.scalar.activation(exp_adj_t[:, jt, :], work_bank(("exp_t", jt)),
                                         ACT.Copy).then_inc(act_work, 1)
                act.wait_ge(pair_ring.filled, b * pair_ring.per_batch)
                turn_features(b, 0)
                gat_factors(b, 0)
                for n in range(H // 2):
                    pair_ring.wait_filled(act, b, ("g", n))
                    nc.scalar.activation(g_all[:, 2 * n:2 * n + 2, :], pair_banks(("g", n)),
                                         ACT.Copy).then_inc(act_pair, 1)
                turn_features(b, 1)
                gat_factors(b, 1)
                pair_ring.wait_filled(act, b, ("g2",))
                nc.scalar.activation(g_one[:], pair_banks(("g2",))[:, 0, :], ACT.Copy).then_inc(act_pair, 1)
                turn_features(b, 2)
                act.wait_ge(stacks_loaded, b * 16 * STACK_DMAS)
                act.wait_ge(qk_split, b)
                for name, whole, high, bias, scale in (("q", q_f32, q_hi, 2, SCALE), ("k", k_f32, k_hi, 1, 1.0)):
                    for m in range(KT):
                        key = (name, m)
                        work_ring.wait_filled(act, b, key)
                        nc.scalar.activation(whole[:, m, :], work_bank(key), ACT.Identity,
                                             bias=qk_bias[:, bias, m:m + 1], scale=scale)
                        nc.scalar.activation(high[:, m, :], work_bank(key), ACT.Identity,
                                             bias=qk_bias[:, bias, m:m + 1], scale=scale).then_inc(act_work, 1)
                work_ring.wait_filled(act, b, ("ac",))
                bank = work_bank(("ac",))
                nc.scalar.activation(ac_f32[:], bank[0:64, :], ACT.Identity, bias=bg[:])
                nc.scalar.activation(ac_hi[:], bank[0:64, :], ACT.Identity, bias=bg[:]).then_inc(act_work, 1)
                act.wait_ge(max_loaded, b * 16)
                work_ring.wait_filled(act, b, ("max_t",))
                nc.scalar.activation(max_t[:], work_bank(("max_t",))[0:H, :], ACT.Copy).then_inc(act_work, 1)
                for q in range(QUADS):
                    for jt in range(IT):
                        u = ("att", q, jt)
                        wait_probs_free(act, b, u)
                        for hp in range(2):
                            key = ("score", q, jt, hp)
                            pair_ring.wait_filled(act, b, key)
                            nc.scalar.activation(probs[:, use(u) % PBUFS, 2 * hp:2 * hp + 2, :], pair_banks(key),
                                                 ACT.Exp).then_inc(act_pair, 1)

        @block.vector
        def _(dve):
            dve.wait_ge(consts_made, CONSTS)
            nc.vector.tensor_copy(select_head[:], select_f32).then_inc(rounded_selector, 1)
            nc.vector.tensor_copy(ones_r, ones_f32).then_inc(rounded_consts, 1)
            nc.vector.tensor_copy(minus_head, minus_head_f32).then_inc(rounded_consts, 1)
            nc.vector.memset(g_hl[:].bitcast(F32), 0.0)
            nc.vector.memset(wa1[:], 0.0)
            nc.vector.memset(wa2[:], 0.0).then_inc(vec_cleared, 1)
            dve.wait_ge(weights_loaded, 16 * N_WEIGHT_LOADS)
            dve.wait_ge(vec_cleared, 1)
            n = 0
            for layer, (w, wa, heads) in enumerate(((w1, wa1, H), (w2, wa2, 1))):
                for side in range(2):
                    for k in range(KT):
                        dve.wait_ge(wa_ready, n)
                        nc.vector.tensor_tensor(wa_tmp, w[:, k, :], a_rows[:, 2 * layer + side, :],
                                                ALU.mult).then_inc(wa_products, 1)
                        dve.wait_ge(wa_products, n + 1)
                        nc.vector.tensor_reduce(wa[:, k, 32 * side:32 * side + heads],
                                                wa_tmp.rearrange("p (h d) -> p h d", h=heads),
                                                AX_X, ALU.add).then_inc(wa_ready, 1)
                        n += 1

            def batch(b):
                step = [0]

                def settle(ins, apart=False):
                    step[0] += 1
                    ins.then_inc(vec_step, 1)
                    dve.wait_ge(vec_step, b * VEC_STEPS + step[0])
                    if apart:
                        nc.vector.memset(spare[:], 0.0)

                def layer_norm(layer, rows):
                    for it in range(IT):
                        ins = nc.vector.bn_stats(stats[:, it, :], rows[:, it, :])
                    settle(ins, apart=True)
                    for it in range(IT):
                        ins = nc.vector.bn_aggr(mean_var[:, it, :], stats[:, it, :])
                    settle(ins)
                    nc.vector.tensor_scalar(var_eps[:, layer, :], mean_var[:, :, 1], LN_EPS, None,
                                            ALU.add).then_inc(var_ready, 1)
                    dve.wait_ge(rstd_ready, b * 2 + layer + 1)
                    for it in range(IT):
                        nc.vector.tensor_scalar(normed[:, it, :], rows[:, it, :], mean_var[:, it, 0:1],
                                                rstd[:, layer, it:it + 1], ALU.subtract,
                                                ALU.mult).then_inc(normed_ready, 1)

                def gat_rows(layer):
                    heads = H if layer == 0 else 1
                    key = ("st", layer)
                    work_ring.wait_filled(dve, b, key)
                    bank = work_bank(key)
                    nc.vector.tensor_copy(s_row[0:heads, :], bank[0:heads, :])
                    nc.vector.tensor_copy(t_row[0:heads, :], bank[32:32 + heads, :]).then_inc(dve_work, 1)
                    work_ring.wait_emptied(dve, b, key)
                    settle(nc.vector.tensor_reduce(t_max[0:heads, layer, 0:1], t_row[0:heads, :],
                                                   AX_X, ALU.max))
                    nc.vector.tensor_scalar(t_max[0:heads, layer, 1:2], t_max[0:heads, layer, 0:1],
                                            1.0 - SLOPE, None, ALU.mult)
                    nc.vector.tensor_scalar(z_row[0:heads, :], t_row[0:heads, :],
                                            t_max[0:heads, layer, 0:1], None,
                                            ALU.subtract).then_inc(st_rows_ready, 1)
                    dve.wait_ge(exp_rows_ready, b * 2 + layer + 1)
                    settle(nc.vector.tensor_copy(g_hl[0:heads, :], g_row[0:heads, :]))
                    nc.vector.tensor_tensor(g_hl[32:32 + heads, :], g_row[0:heads, :],
                                            g_hl[0:heads, :].bitcast(F32),
                                            ALU.subtract).then_inc(g_split, 1)

                def normalise_heads(kind, layer, q):
                    dve.wait_ge(probs_used, b * NPU + use((kind, q, IT - 1)) + 1)
                    settle(nc.vector.reciprocal(recip[:], heads_ps[:, 1, :]))
                    nc.vector.tensor_tensor(heads_t[:, layer, q, :], heads_ps[:, 0, :], recip[:],
                                            ALU.mult).then_inc(heads_emptied, 1)

                dve.wait_ge(adj_loaded, b * 16 + 16)
                dve.wait_ge(exp_adj_ready, b * IT)
                nc.vector.tensor_reduce(neg_adj_max[:], adj_rows[:], AX_X, ALU.max,
                                        negate=True).then_inc(adj_max_ready, 1)
                dve.wait_ge(x_loaded, b * 16 + 16)
                dve.wait_ge(stored, b * 16)
                layer_norm(0, x_rows)
                gat_rows(0)
                work_ring.wait_emptied(dve, b, ("cols", 0))
                factor = c_cols[:, 0, :, 0:H].rearrange("p t (h a) -> p t h a", a=1).broadcast_to((P, IT, H, DH))
                nc.vector.tensor_copy(d1[:], factor)
                pair_ring.wait_filled(dve, b, ("h", 0))
                nc.vector.tensor_tensor(v1[:], pair_rows(("h", 0)).rearrange("p t (h d) -> p t h d", h=H),
                                        factor, ALU.mult).then_inc(dve_pair, 1)
                for q in range(QUADS):
                    for jt in range(IT):
                        u = ("gat1", q, jt)
                        if jt == 0:
                            pair_ring.wait_emptied(dve, b, ("g", 2 * q + 1))
                        if q == 0:
                            work_ring.wait_emptied(dve, b, ("exp_t", jt))
                        wait_probs_free(dve, b, u)
                        for g in range(4):
                            h = 4 * q + g
                            ins = nc.vector.scalar_tensor_tensor(
                                probs[:, use(u) % PBUFS, g, :], g_all[:, h, :], c_cols[:, 0, jt, 32 + h:33 + h],
                                exp_adj_t[:, jt, :], ALU.max, ALU.mult)
                        ins.then_inc(probs_dve, 1)
                        if q == 1 and jt == 0:
                            normalise_heads("gat1", 0, 0)
                normalise_heads("gat1", 0, 1)
                pair_ring.wait_filled(dve, b, ("back", 0))
                nc.vector.tensor_tensor(x2[:], pair_rows(("back", 0)), x_rows[:],
                                        ALU.add).then_inc(dve_pair, 1)
                pair_ring.wait_emptied(dve, b, ("back", 0))
                layer_norm(1, x2)
                gat_rows(1)
                work_ring.wait_emptied(dve, b, ("cols", 1))
                nc.vector.tensor_copy(v2[:, :, D:D + 2], c_cols[:, 1, :, 0:1].broadcast_to((P, IT, 2)))
                pair_ring.wait_filled(dve, b, ("h", 1))
                nc.vector.tensor_tensor(v2[:, :, 0:D], pair_rows(("h", 1)),
                                        c_cols[:, 1, :, 0:1].broadcast_to((P, IT, D)),
                                        ALU.mult).then_inc(dve_pair, 1)
                pair_ring.wait_emptied(dve, b, ("g2",))
                u = ("gat2", 0, 0)
                wait_probs_free(dve, b, u)
                for jt in range(IT):
                    ins = nc.vector.scalar_tensor_tensor(
                        probs[:, use(u) % PBUFS, jt, :], g_one[:], c_cols[:, 1, jt, 32:33],
                        exp_adj_t[:, jt, :], ALU.max, ALU.mult)
                ins.then_inc(probs_dve, 1)
                for it in range(IT):
                    if it < IT - 1:
                        dve.wait_ge(rows_filled, b * (IT - 1) + it + 1)
                    else:
                        dve.wait_ge(probs_used, b * NPU + use(u) + 1)
                    settle(nc.vector.reciprocal(recip1[:, it:it + 1], heads_ps[:, it % 2, D:D + 1]))
                    nc.vector.scalar_tensor_tensor(x3[:, it, :], heads_ps[:, it % 2, 0:D], recip1[:, it:it + 1],
                                                   x2[:, it, :], ALU.mult, ALU.add).then_inc(heads_emptied, 1)
                dve.wait_ge(stacks_loaded, b * 16 * STACK_DMAS)
                for name, whole, high, low in (("q", q_f32, q_hi, q_lo), ("k", k_f32, k_hi, k_lo)):
                    for m in range(KT):
                        work_ring.wait_emptied(dve, b, (name, m))
                        nc.vector.tensor_tensor(low[:, m, :], whole[:, m, :], high[:, m, :].bitcast(F32),
                                                ALU.subtract)
                work_ring.wait_emptied(dve, b, ("ac",))
                nc.vector.tensor_tensor(ac_lo[:], ac_f32[:], ac_hi[:].bitcast(F32),
                                        ALU.subtract).then_inc(qk_split, 1)
                pair_ring.wait_filled(dve, b, ("v",))
                nc.vector.tensor_tensor(v3, pair_rows(("v",)),
                                        bv[:].rearrange("p (a d) -> p a d", a=1).broadcast_to((P, IT, D)),
                                        ALU.add).then_inc(dve_pair, 1)
                for h in range(H):
                    for ip in range(IT // 2):
                        key = ("max", h, ip)
                        pair_ring.wait_filled(dve, b, key)
                        nc.vector.tensor_reduce(row_max[:, 2 * ip:2 * ip + 2, h:h + 1], pair_banks(key),
                                                AX_X, ALU.max).then_inc(dve_pair, 1)
                for q in range(QUADS):
                    for jt in range(IT):
                        u = ("att", q, jt)
                        if u in dve_uses:
                            pair_ring.wait_emptied(dve, b, ("score", q, jt, 1))
                            p = probs[:, use(u) % PBUFS, :, :]
                            nc.vector.tensor_tensor(p, p, adj_t[:, jt:jt + 1, :].broadcast_to((P, 4, N)),
                                                    ALU.mult).then_inc(probs_dve, 1)
                        if q == 1 and jt == 0:
                            normalise_heads("att", 1, 0)
                normalise_heads("att", 1, 1)
                pair_ring.wait_filled(dve, b, ("back", 1))
                nc.vector.tensor_tensor(out_rows[:], pair_rows(("back", 1)), x3[:],
                                        ALU.add).then_inc(dve_pair, 1)
                return step[0]

            with dve.Fori(0, B) as b:
                steps = batch(b)
            assert steps == VEC_STEPS, steps

        @block.tensor
        def _(pe):
            pe.wait_ge(consts_made, CONSTS)
            pe.wait_ge(rounded_selector, 1)
            pe.wait_ge(wa_ready, 8)
            pe.wait_ge(stack_consts, 16 * (2 + N // P))
            pe.wait_ge(vec_cleared, 1)

            def turn_rows(b, layer):
                for m in range(KT):
                    key = ("feat", layer, m)
                    work_ring.wait_free(pe, b, key)
                    for it in range(IT):
                        if m == 0 and layer < 2:
                            pe.wait_ge(normed_ready, b * 2 * IT + layer * IT + it + 1)
                        if m == 0 and layer == 2:
                            pe.wait_ge(heads_emptied, b * HEAD_USES + QUADS + it + 1)
                        rows = normed if layer < 2 else x3
                        mm = nc.tensor.transpose(work_bank(key)[:, it * P:(it + 1) * P],
                                                 rows[:, it, m * P:(m + 1) * P], ident[:])
                    mm.then_inc(work_ring.filled, 1)

            def project_rows(b, layer, w, key):
                pair_ring.wait_free(pe, b, key)
                for t in range(IT):
                    for k in range(KT):
                        mm = nc.tensor.matmul(pair_rows(key)[:, t, :], feat_t[:, layer % 2, k, t * P:(t + 1) * P],
                                              w[:, k, :], start=(k == 0), stop=(k == KT - 1))
                mm.then_inc(pair_ring.filled, 1)

            def gat_scores(b, layer, wa):
                key = ("st", layer)
                work_ring.wait_free(pe, b, key)
                for k in range(KT):
                    work_ring.wait_emptied(pe, b, ("feat", layer, k))
                    mm = nc.tensor.matmul(work_bank(key)[0:64, :], wa[:, k, :], feat_t[:, layer % 2, k, :],
                                          start=(k == 0), stop=(k == KT - 1))
                mm.then_inc(work_ring.filled, 1)

            def gat_columns(b, layer):
                key = ("cols", layer)
                work_ring.wait_free(pe, b, key)
                pe.wait_ge(exp_rows_ready, b * 2 + layer + 1)
                for jt in range(IT):
                    mm = nc.tensor.transpose(work_bank(key)[:, P * jt:P * jt + P],
                                             c_rows[:, jt * P:(jt + 1) * P], ident[:])
                mm.then_inc(work_ring.filled, 1)

            def values(b, n, kind, q, value, weight):
                pe.wait_ge(heads_emptied, b * HEAD_USES + n)
                for jt in range(IT):
                    values_of(b, kind, q, jt, value, weight)

            def values_of(b, kind, q, jt, value, weight):
                    u = (kind, q, jt)
                    uses, made = (pool_uses, probs_pool) if u in pool_uses else (dve_uses, probs_dve)
                    pe.wait_ge(made, b * len(uses) + uses.index(u) + 1)
                    for bank, stationary in enumerate((value, weight)):
                        for g in range(4):
                            mm = nc.tensor.matmul(heads_ps[32 * g:32 * g + 32, bank, :], stationary(jt, 4 * q + g),
                                                  probs[:, use(u) % PBUFS, g, :], start=(jt == 0),
                                                  stop=(jt == IT - 1), tile_position=(0, 32 * g))
                    mm.then_inc(probs_used, 1)

            def turn_back(b, layer, key):
                pair_ring.wait_free(pe, b, key)
                for m in range(QUADS):
                    pe.wait_ge(heads_emptied, b * HEAD_USES + (m + 1 if layer == 0 else QUADS + IT + m + 1))
                    for it in range(IT):
                        mm = nc.tensor.transpose(pair_rows(key)[:, it, m * P:(m + 1) * P],
                                                 heads_t[:, layer, m, it * P:(it + 1) * P], ident[:])
                mm.then_inc(pair_ring.filled, 1)

            def scores(b, key):
                _, q, jt, hp = key
                pair_ring.wait_free(pe, b, key)
                for n in range(2):
                    h = 4 * q + 2 * hp + n
                    mm = nc.tensor.matmul(pair_banks(key)[:, n, :], k_stack[:, h, jt * P:(jt + 1) * P],
                                          q_stack[:, h, :], start=True, stop=True)
                mm.then_inc(pair_ring.filled, 1)

            with pe.Fori(0, B) as b:
                pe.wait_ge(adj_loaded, b * 16 + 16)
                for name, rows in (("adj_t", adj_rows), ("exp_t", exp_adj)):
                    if name == "exp_t":
                        pe.wait_ge(exp_adj_ready, b * IT + IT)
                    for jt in range(IT):
                        key = (name, jt)
                        work_ring.wait_free(pe, b, key)
                        for it in range(IT):
                            mm = nc.tensor.transpose(work_bank(key)[:, it * P:(it + 1) * P],
                                                     rows[:, it, jt * P:(jt + 1) * P], ident[:])
                        mm.then_inc(work_ring.filled, 1)

                turn_rows(b, 0)
                gat_scores(b, 0, wa1)
                project_rows(b, 0, w1, ("h", 0))
                gat_columns(b, 0)
                pe.wait_ge(g_split, b * 2 + 1)
                for n in range(H // 2):
                    key = ("g", n)
                    pair_ring.wait_free(pe, b, key)
                    for a in range(2):
                        mm = nc.tensor.matmul(pair_banks(key)[:, a, :], select_head[:, 2 * n + a, :],
                                              g_hl[:], start=True, stop=True)
                    mm.then_inc(pair_ring.filled, 1)
                pair_ring.wait_emptied(pe, b, ("h", 0))
                for q in range(QUADS):
                    values(b, q, "gat1", q, lambda jt, h: v1[:, jt, h, :], lambda jt, h: d1[:, jt, h, :])
                turn_back(b, 0, ("back", 0))

                turn_rows(b, 1)
                gat_scores(b, 1, wa2)
                project_rows(b, 1, w2, ("h", 1))
                gat_columns(b, 1)
                pe.wait_ge(g_split, b * 2 + 2)
                pair_ring.wait_free(pe, b, ("g2",))
                nc.tensor.matmul(pair_banks(("g2",))[:, 0, :], select_head[:, 0, :], g_hl[:],
                                 start=True, stop=True).then_inc(pair_ring.filled, 1)
                pair_ring.wait_emptied(pe, b, ("h", 1))
                u = ("gat2", 0, 0)
                pe.wait_ge(probs_dve, b * len(dve_uses) + dve_uses.index(u) + 1)
                for it in range(IT):
                    pe.wait_ge(heads_emptied, b * HEAD_USES + QUADS + max(it - 1, 0))
                    for jt in range(IT):
                        mm = nc.tensor.matmul(heads_ps[:, it % 2, 0:D + 2],
                                              probs[:, use(u) % PBUFS, jt, it * P:(it + 1) * P],
                                              v2[:, jt, 0:D + 2], start=(jt == 0), stop=(jt == IT - 1))
                    mm.then_inc(rows_filled if it < IT - 1 else probs_used, 1)

                turn_rows(b, 2)
                for k in range(KT):
                    work_ring.wait_emptied(pe, b, ("feat", 2, k))
                for name, w in (("q", wq), ("k", wk)):
                    for m in range(KT):
                        key = (name, m)
                        work_ring.wait_free(pe, b, key)
                        for k in range(KT):
                            mm = nc.tensor.matmul(work_bank(key), w[:, k, m * P:(m + 1) * P],
                                                  feat_t[:, 0, k, :], start=(k == 0), stop=(k == KT - 1))
                        mm.then_inc(work_ring.filled, 1)
                key = ("ac",)
                work_ring.wait_free(pe, b, key)
                for k in range(KT):
                    mm = nc.tensor.matmul(work_bank(key)[0:64, :], wg[:, k, :], feat_t[:, 0, k, :],
                                          start=(k == 0), stop=(k == KT - 1))
                mm.then_inc(work_ring.filled, 1)
                project_rows(b, 2, wv, ("v",))

                pe.wait_ge(stacks_loaded, (b + 1) * 16 * STACK_DMAS)
                for h in range(H):
                    for ip in range(IT // 2):
                        key = ("max", h, ip)
                        pair_ring.wait_free(pe, b, key)
                        for n in range(2):
                            it = 2 * ip + n
                            mm = nc.tensor.matmul(pair_banks(key)[:, n, :], q_stack[0:104, h, it * P:(it + 1) * P],
                                                  k_stack[0:104, h, :], start=True, stop=True)
                        mm.then_inc(pair_ring.filled, 1)
                pair_ring.wait_emptied(pe, b, ("max", H - 1, IT // 2 - 1))
                key = ("max_t",)
                work_ring.wait_free(pe, b, key)
                for it in range(IT):
                    mm = nc.tensor.transpose(work_bank(key)[0:H, it * P:(it + 1) * P], row_max[:, it, :], ident[:])
                mm.then_inc(work_ring.filled, 1)
                pe.wait_ge(max_loaded, b * 16 + 16)

                pair_ring.wait_emptied(pe, b, ("v",))
                steps = [(q, jt) for q in range(QUADS) for jt in range(IT)]
                for n in range(len(steps) + 1):
                    if n < len(steps):
                        for hp in range(2):
                            scores(b, ("score", *steps[n], hp))
                    if n > 0:
                        q, jt = steps[n - 1]
                        if jt == 0:
                            pe.wait_ge(heads_emptied, b * HEAD_USES + QUADS + IT + q)
                        values_of(b, "att", q, jt, lambda jt, h: v3[:, jt, h * DH:(h + 1) * DH],
                                  lambda jt, h: ones[:])
                turn_back(b, 1, ("back", 1))


_INS = ["x", "adj", "L0_gnn_W1", "L0_gnn_a_src1", "L0_gnn_a_dst1", "L0_gnn_g1", "L0_gnn_b1", "L0_gnn_W2",
        "L0_gnn_a_src2", "L0_gnn_a_dst2", "L0_gnn_g2", "L0_gnn_b2", "L1_gnn_W_q", "L1_gnn_b_q", "L1_gnn_W_k",
        "L1_gnn_b_k", "L1_gnn_W_v", "L1_gnn_b_v", "L1_gnn_w_g", "L1_gnn_b_g"]


def kernel(**inputs):
    import numpy as _np
    import concourse.bacc as _bacc
    from concourse import mybir as _mybir
    from concourse.bass_utils import run_bass_kernel_spmd as _run

    nc = _bacc.Bacc("TRN2", target_bir_lowering=False, num_devices=1)
    arrays, args = {}, []
    for name in _INS:
        a = _np.ascontiguousarray(inputs[name])
        if a.ndim == 0:
            a = a.reshape(1)
        arrays[f"in_{name}_dram"] = a
        args.append(nc.dram_tensor(f"in_{name}_dram", a.shape, _mybir.dt.from_np(a.dtype), kind="ExternalInput").ap())
    shape = inputs["x"].shape
    args.append(nc.dram_tensor("out_0_dram", shape, _mybir.dt.float32, kind="ExternalOutput").ap())
    two_gat_layers_then_biased_attention(nc, *args)
    r = _run(nc, [arrays], core_ids=[0])
    return r.results[0]["out_0_dram"]
```

```python
from contextlib import ExitStack

import concourse.bass as bass
from concourse import mybir

F32 = mybir.dt.float32
F32R = mybir.dt.float32r
ALU = mybir.AluOpType
ACT = mybir.ActivationFunctionType
AX_X = mybir.AxisListType.X

P = 128
START = 3


class Batch:

    def __init__(self, register, shift=0):
        self.register, self.shift = register, shift

    def count(self, per_batch, more=0):
        return self.register * per_batch + (self.shift * per_batch + more + START)


class Banks:

    def __init__(self, fills, size, filled, emptied):
        self.fills, self.size, self.filled, self.emptied = fills, size, filled, emptied
        self.number = {key: n for n, (key, _) in enumerate(fills)}
        self.by = {key: engine for key, engine in fills}
        self.total = {e: sum(engine == e for _, engine in fills) for e in emptied}

    def bank(self, key):
        return self.number[key] % self.size

    def fill_count(self, b, key):
        return b.count(len(self.fills), self.number[key] + 1)

    def empty_count(self, b, key):
        e = self.by[key]
        return b.count(self.total[e], sum(engine == e for _, engine in self.fills[:self.number[key] + 1]))

    def wait_filled(self, eng, b, key):
        eng.wait_ge(self.filled, self.fill_count(b, key))

    def wait_emptied(self, eng, b, key):
        eng.wait_ge(self.emptied[self.by[key]], self.empty_count(b, key))

    def wait_free(self, pe, b, key):
        n = self.number[key] - self.size
        if n >= 0:
            self.wait_emptied(pe, b, self.fills[n][0])
        else:
            last = max(m for m in range(len(self.fills)) if m % self.size == self.bank(key))
            later = [engine for _, engine in self.fills[last:]]
            pe.wait_ge(self.emptied[later[0]], b.count(self.total[later[0]], 1 - later.count(later[0])))


def two_gat_layers_then_biased_attention(
    nc, x, adj, W1, a_src1, a_dst1, g1, b1, W2, a_src2, a_dst2, g2, b2,
    W_q, b_q, W_k, b_k, W_v, b_v, w_g, b_g, out,
):
    B, N, D = x.shape
    H, DH = a_src1.shape
    IT = N // P
    KT = D // P
    QUADS = H // 4
    HALF = DH // QUADS
    SCALE = float(DH) ** -0.5
    LN_EPS = 1e-6
    ADJ_EPS = 1e-9
    SLOPE = 0.2
    A_BUFS, B_BUFS = 2, 3
    assert DH == 32 and D == 256 and N == 512 and KT == QUADS == 2

    STEPS = [(q, jt) for q in range(QUADS) for jt in range(IT)]
    NS = len(STEPS)
    DVE_STEPS = [4, 6, 7]
    POOL_STEPS = [n for n in range(NS) if n not in DVE_STEPS]
    A_PROBS = NS + 1
    AHEAD = 6

    with ExitStack() as ctx:
        def sb(name, shape, dt=F32):
            return ctx.enter_context(nc.sbuf_tensor(name, shape, dt))

        def ps(name, shape):
            return ctx.enter_context(nc.psum_tensor(name, shape, F32))

        ident = sb("ident", [P, P])
        select_head = sb("select_head", [P, H, P], F32R)
        ones = sb("ones", [P, QUADS, DH])
        minus_half = sb("minus_half", [P, IT])
        w1 = sb("w1", [P, KT, D])
        w2 = sb("w2", [P, KT, D])
        wq = sb("wq", [P, KT, D])
        wk = sb("wk", [P, KT, D])
        wv = sb("wv", [P, KT, D])
        wg = sb("wg", [P, KT, 64])
        wa1 = sb("wa1", [P, KT, 64])
        wa2 = sb("wa2", [P, KT, 64])
        gb = sb("gb", [P, 4, KT])
        qk_bias = sb("qk_bias", [P, 3, KT])
        bv = sb("bv", [P, D])
        bg = sb("bg", [64, 1])

        x_rows = sb("x_rows", [P, IT, D])
        adj_rows = sb("adj_rows", [P, IT, N])
        neg_adj_max = sb("neg_adj_max", [P, IT])
        exp_adj_t = sb("exp_adj_t", [P, IT, N])
        stats = sb("stats", [P, IT, 6])
        mean_var = sb("mean_var", [P, IT, 2])
        var_eps = sb("var_eps", [P, 2, IT])
        rstd = sb("rstd", [P, 2, IT])
        spare = sb("spare", [P, 1])
        normed = sb("normed", [P, IT, D])
        feat_a = sb("feat_a", [P, KT, N])
        t_max = sb("t_max", [64, 4])
        g_hl = sb("g_hl", [P, N], F32R)
        fc_rows = sb("fc_rows", [P, N])
        fc_cols = sb("fc_cols", [P, 2, IT, 64])
        g_all = sb("g_all", [P, H, N])
        v1 = sb("v1", [P, IT, H, DH])
        c1 = sb("c1", [P, IT, H, DH])
        v2 = sb("v2", [P, IT, D + 2])
        probs_a = sb("probs_a", [P, A_BUFS, 4, N])
        exp_adj = probs_a[:, 1, :, :]
        num_a = normed[:].rearrange("p (q r) d -> p q (r d)", q=QUADS)
        den_a = sb("den_a", [P, N])
        g_2 = den_a
        recip_a = sb("recip_a", [P, IT, QUADS, 4])
        recip_2 = sb("recip_2", [P, IT])
        x2 = sb("x2", [P, IT, D])

        adj_t = sb("adj_t", [P, IT, N])
        x3 = sb("x3", [P, IT, D])

        feat_b = sb("feat_b", [P, KT, N])
        v3 = sb("v3", [P, IT, D])
        qk_f32 = sb("qk_f32", [P, KT, N])
        out_rows = qk_f32[:].rearrange("p k (c d) -> p (k c) d", d=D)
        normed_1 = out_rows
        q_hi = sb("q_hi", [P, KT, N], F32R)
        q_lo = sb("q_lo", [P, KT, N], F32R)
        k_hi = sb("k_hi", [P, KT, N], F32R)
        k_lo = sb("k_lo", [P, KT, N], F32R)
        ac_f32 = sb("ac_f32", [64, N])
        ac_parts = sb("ac_parts", [P, N], F32R)
        ac_hi, ac_lo = ac_parts[0:64, :], ac_parts[64:P, :]
        row_max = sb("row_max", [P, IT, H])
        max_t = sb("max_t", [4, QUADS, N], F32R)
        q_stack = sb("q_stack", [P, H, N], F32R)
        k_stack = sb("k_stack", [P, H, N], F32R)
        probs_b = sb("probs_b", [P, B_BUFS, 4, N])
        num_b = q_hi[:].bitcast(F32)
        den_b = q_lo[:, 0, :].bitcast(F32)
        recip_b = sb("recip_b", [P, IT, QUADS, 4])

        select_f32 = probs_b[:, 0, 0:2, :].rearrange("p a (c n) -> p (a c) n", n=P)
        a_rows = probs_b[:, 0, 2:4, :].rearrange("p a (c n) -> p (a c) n", n=D)
        minus_head_f32 = probs_b[0:H, 1, 0:2, :].rearrange("p a (c n) -> p (a c) n", n=P)
        minus_head = probs_b[0:H, 1, 2:4, :].rearrange("p a (c n) -> p (a c) n", n=P)
        ones_row = probs_b[0:2, 2, 0, :]
        wa_tmp = probs_b[:, 2, 2, 0:D]

        heads_a = ps("heads_a", [P, 2, N])
        heads_b = ps("heads_b", [P, 2, N])
        ring_a = ps("ring_a", [P, 2, N])
        ring_b = ps("ring_b", [P, 2, N])

        def sem(name):
            return ctx.enter_context(nc.semaphore(name))

        weights_loaded = sem("weights_loaded")
        consts_made = sem("consts_made")
        rounded_consts = sem("rounded_consts")
        stack_consts = sem("stack_consts")
        wa_products = sem("wa_products")
        wa_ready = sem("wa_ready")
        vec_cleared = sem("vec_cleared")
        scaled_bias = sem("scaled_bias")

        loop_sems = []

        def counted(name):
            loop_sems.append(sem(name))
            return loop_sems[-1]

        x_loaded = counted("x_loaded")
        adj_loaded = counted("adj_loaded")
        adj_loaded_again = counted("adj_loaded_again")
        stacks_loaded = counted("stacks_loaded")
        max_loaded = counted("max_loaded")
        stored = counted("stored")
        adj_max_ready = counted("adj_max_ready")
        exp_adj_ready = counted("exp_adj_ready")
        var_ready = counted("var_ready")
        rstd_ready = counted("rstd_ready")
        normed_ready = counted("normed_ready")
        t_max_ready = counted("t_max_ready")
        exp_rows_ready = counted("exp_rows_ready")
        g_split = counted("g_split")
        probs_a_ready = counted("probs_a_ready")
        probs_a_used = counted("probs_a_used")
        rows2_filled = counted("rows2_filled")
        rows2_emptied = counted("rows2_emptied")
        heads_a_emptied = counted("heads_a_emptied")
        x2_ready = counted("x2_ready")
        x3_ready = counted("x3_ready")
        parts_split = counted("parts_split")
        probs_b_vec = counted("probs_b_vec")
        probs_b_pool = counted("probs_b_pool")
        probs_b_used = counted("probs_b_used")
        heads_b_emptied = counted("heads_b_emptied")
        out_ready = counted("out_ready")
        stats_ready = counted("stats_ready")
        mean_ready = counted("mean_ready")
        target_max_found = counted("target_max_found")
        recip_2_ready = counted("recip_2_ready")

        front_fills = [(("feat", 0, m), "act") for m in range(KT)] + [(("st", 0), "act")] \
            + [(("exp_t", jt), "act") for jt in range(IT)] + [(("cols", 0), "act")] \
            + [(("g", h), "act") for h in range(4)] + [(("h", 0, n), "vec") for n in range(2)] \
            + [(("g", h), "act") for h in range(4, H)]
        A = Banks(
            [(("den",), "vec")] + [(("back", n), "vec") for n in range(2)]
            + [(("feat", 1, m), "act") for m in range(KT)] + [(("st", 1), "act")]
            + [(("h", 1, n), "vec") for n in range(2)] + [(("cols", 1), "act"), (("g2",), "act")]
            + front_fills + [(("adj_t", jt), "act") for jt in range(IT)],
            2, counted("a_filled"), {"act": counted("a_emptied_act"), "vec": counted("a_emptied_vec")})
        A0 = Banks(front_fills, 2, counted("first_filled"),
                   {"act": counted("first_emptied_act"), "vec": counted("first_emptied_vec")})
        def max_fills(heads):
            return [(("max", h, it), "vec") for h in heads for it in range(IT)]

        def score_fills(steps):
            return [(("score", n, g), "act") for n in steps for g in range(4)]

        MAX_AND_SCORES = max_fills(range(4)) + [(("max_t", 0), "act")] + max_fills((4,)) + score_fills((0,)) \
            + max_fills((5,)) + score_fills((1,)) + max_fills((6,)) + score_fills((2,)) + max_fills((7,)) \
            + [(("max_t", 1), "act")] + score_fills(range(3, NS))
        Bb = Banks(
            [(("feat", m), "act") for m in range(KT)] + [(("q", m), "act") for m in range(KT)]
            + [(("k", m), "act") for m in range(KT)] + [(("ac",), "act")] + [(("v", n), "vec") for n in range(2)]
            + MAX_AND_SCORES
            + [(("den",), "vec")] + [(("back", n), "vec") for n in range(2)],
            2, counted("b_filled"), {"act": counted("b_emptied_act"), "vec": counted("b_emptied_vec")})

        def bank_a(ring, key):
            return ring_a[:, ring.bank(key), :]

        def bank_b(key):
            return ring_b[:, Bb.bank(key), :]

        def as_rows(bank):
            return bank.rearrange("p (t d) -> p t d", d=D)

        def as_heads(rows):
            return rows.rearrange("p t (h d) -> p t h d", d=DH)

        def by_feature(w):
            return w.rearrange("(k p) n -> p k n", p=P)

        def column(v):
            return v.rearrange("(k p) -> p k", p=P)

        weight_loads = [(w1[:], by_feature(W1)), (w2[:], by_feature(W2)), (wq[:], by_feature(W_q)),
                        (wk[:], by_feature(W_k)), (wv[:], by_feature(W_v))]
        weight_loads += [(gb[:, n, :], column(v)) for n, v in enumerate((g1, b1, g2, b2))]
        weight_loads += [(qk_bias[:, n, :], column(v)) for n, v in enumerate((b_q, b_k))]
        weight_loads += [(a_rows[:, n, :], v.rearrange("h d -> (h d)").partition_broadcast(P))
                         for n, v in enumerate((a_src1, a_dst1, a_src2, a_dst2))]
        weight_loads += [(bv[:], b_v.partition_broadcast(P))]
        gate = w_g.rearrange("(s k p) -> p s k", p=P, k=KT)
        late_loads = [(bg[0:1, :], b_g.rearrange("(a b) -> a b", a=1))]
        late_loads += [(wg[:, k, 32 * s:32 * s + 1], gate[:, s, k:k + 1]) for s in range(2) for k in range(KT)]
        N_WEIGHT_LOADS = len(weight_loads) + len(late_loads)
        CONSTS = 18
        STACK_DMAS = 4 * 6 + 4
        VEC_STEPS = 2 * (2 + 1) + IT

        x_tiles = x.rearrange("b (t p) d -> b p t d", p=P)
        adj_tiles = adj.rearrange("b (t p) n -> b p t n", p=P)
        out_tiles = out.rearrange("b (t p) d -> b p t d", p=P)

        def loop(eng, first, pair, last):
            first(Batch(0), Batch(0, 1))
            with eng.Fori(0, B - 1) as i:
                pair(Batch(i, 2), Batch(i, 1), Batch(i))
            last(Batch(B - 1))

        block = ctx.enter_context(nc.Block())

        @block.sync
        def _(sp):
            for s in loop_sems:
                sp.sem_inc(s, START)
            for dst, src in weight_loads:
                sp.dma_start(dst, src, allow_slow_non_contiguous=True).then_inc(weights_loaded, 16)
            sp.dma_start(adj_rows[:], adj_tiles[0]).then_inc(adj_loaded, 16)
            sp.dma_start(x_rows[:], x_tiles[0]).then_inc(x_loaded, 16)
            sp.wait_ge(consts_made, CONSTS)
            for dst, src in late_loads:
                sp.dma_start(dst, src, allow_slow_non_contiguous=True).then_inc(weights_loaded, 16)
            q_raw, k_raw = q_stack[:].bitcast(F32), k_stack[:].bitcast(F32)
            sp.dma_start(k_raw[96:98, :, :], ones_row.unsqueeze(1).broadcast_to((2, H, N))).then_inc(stack_consts, 16)
            sp.dma_start(q_raw[98:100, :, :], ones_row.unsqueeze(1).broadcast_to((2, H, N))).then_inc(stack_consts, 16)
            for n in range(N // P):
                sp.dma_start(k_raw[104:104 + H, :, n * P:(n + 1) * P], minus_head_f32).then_inc(stack_consts, 16)

            def load_x(b, n):
                sp.wait_ge(x2_ready, b.count(IT // 2, IT // 2))
                sp.dma_start(x_rows[:], x_tiles[n]).then_inc(x_loaded, 16)

            def load_adj(n):
                sp.dma_start(adj_rows[:], adj_tiles[n]).then_inc(adj_loaded, 16)

            def load_adj_again(b, after, n):
                sp.wait_ge(exp_adj_ready, after.count(IT, IT))
                sp.dma_start(adj_rows[:], adj_tiles[n]).then_inc(adj_loaded_again, 16)

            def stacks(b):
                for name, rows, parts in (("q", q_raw, (q_hi, q_hi)), ("k", k_raw, (k_hi, None, k_hi))):
                    Bb.wait_emptied(sp, b, (name, KT - 1))
                    for n, part in enumerate(parts):
                        if part is not None:
                            move(rows, n, part)
                sp.wait_ge(parts_split, b.count(2, 2))
                move(q_raw, 2, q_lo)
                move(k_raw, 1, k_lo)
                for n, (rows, part, r) in enumerate(((q_raw, ac_hi, 0), (q_raw, ac_lo, 0),
                                                     (k_raw, ac_hi, 32), (k_raw, ac_lo, 32))):
                    sp.dma_start(rows[96 + n:97 + n, :, :],
                                 part[r:r + 1, :].bitcast(F32).unsqueeze(1).broadcast_to((1, H, N))
                                 ).then_inc(stacks_loaded, 16)

            def move(rows, n, part):
                for g in range(4):
                    sp.dma_start(rows[32 * n:32 * n + 32, g:H:4, :],
                                 part[32 * g:32 * g + 32, :, :].bitcast(F32)).then_inc(stacks_loaded, 16)

            def maxima(b, q):
                Bb.wait_emptied(sp, b, ("max_t", q))
                sp.dma_start(q_raw[104 + 4 * q:108 + 4 * q, 4 * q:4 * q + 4, :],
                             max_t[:, q, :].bitcast(F32).unsqueeze(1).broadcast_to((4, 4, N))
                             ).then_inc(max_loaded, 16)

            def store(b, n):
                sp.wait_ge(out_ready, b.count(IT // 2, IT // 2))
                sp.dma_start(out_tiles[n], out_rows).then_inc(stored, 16)

            sp.wait_ge(exp_adj_ready, Batch(0).count(IT, IT))
            load_adj(1)
            load_x(Batch(0), 1)
            load_adj_again(Batch(0), Batch(1), 0)

            def round_of(n, a, b, into, again, source):
                A.wait_filled(sp, b, ("adj_t", IT - 1))
                load_adj(source)
                stacks(b)
                load_x(a, source)
                load_adj_again(a, n, again)
                maxima(b, 0)
                maxima(b, 1)
                store(b, into)

            with sp.Fori(0, B - 2) as i:
                round_of(Batch(i, 2), Batch(i, 1), Batch(i), i, i + 1, i + 2)
            round_of(Batch(B), Batch(B - 1), Batch(B - 2), B - 2, B - 1, B - 1)
            stacks(Batch(B - 1))
            maxima(Batch(B - 1), 0)
            maxima(Batch(B - 1), 1)
            store(Batch(B - 1), B - 1)
            sp.wait_ge(stored, 16 * B + START)

        @block.gpsimd
        def _(pool):
            for tile, value in ((ident[:], 0.0), (select_f32, 0.0), (minus_head_f32, 0.0), (ones_row, 1.0),
                                (ones[:], 0.0), (minus_half[:], -0.5), (wg[:], 0.0), (bg[:], 0.0),
                                (fc_rows[:], 0.0), (c1[:], 0.0)):
                pool.memset(tile, value).then_inc(consts_made, 1)
            pool.wait_ge(consts_made, 10)
            pool.affine_select(out=ident[:], in_=ident[:], compare_op=ALU.not_equal, fill=1.0, base=0,
                               pattern=[[-1, P]], channel_multiplier=1).then_inc(consts_made, 1)
            pool.affine_select(out=select_f32, in_=select_f32, compare_op=ALU.not_equal, fill=1.0, base=-64,
                               pattern=[[-1, H], [0, P]], channel_multiplier=1).then_inc(consts_made, 1)
            pool.affine_select(out=minus_head_f32, in_=minus_head_f32, compare_op=ALU.not_equal, fill=-1.0,
                               base=0, pattern=[[-1, H], [0, P]], channel_multiplier=1).then_inc(consts_made, 1)
            for q in range(QUADS):
                pool.memset(ones[:, q, q * HALF:(q + 1) * HALF], 1.0).then_inc(consts_made, 1)
            pool.wait_ge(consts_made, 15)
            pool.affine_select(out=select_f32, in_=select_f32, compare_op=ALU.not_equal, fill=1.0, base=-96,
                               pattern=[[-1, H], [0, P]], channel_multiplier=1).then_inc(consts_made, 1)
            for n, rows in enumerate((q_stack, k_stack)):
                pool.wait_ge(consts_made, 16 + n)
                pool.memset(rows[96:P, :, :].bitcast(F32), 0.0).then_inc(consts_made, 1)
            pool.wait_ge(consts_made, CONSTS)

            def inverse_deviation(b, layer):
                pool.wait_ge(var_ready, b.count(2, layer + 1))
                pool.tensor_tensor(rstd[:, layer, :], var_eps[:, layer, :], minus_half[:],
                                   ALU.pow).then_inc(rstd_ready, 1)

            def multiply(b, n):
                Bb.wait_emptied(pool, b, ("score", n, 3))
                p = probs_b[:, n % B_BUFS, :, :]
                jt = STEPS[n][1]
                pool.tensor_tensor(p, p, adj_t[:, jt:jt + 1, :].broadcast_to((P, 4, N)),
                                   ALU.mult).then_inc(probs_b_pool, 1)

            def first(a, n):
                inverse_deviation(a, 0)
                inverse_deviation(a, 1)
                inverse_deviation(n, 0)

            def pair(n, a, b):
                inverse_deviation(a, 1)
                inverse_deviation(n, 0)
                for s in POOL_STEPS:
                    multiply(b, s)

            def last(b):
                for n in POOL_STEPS:
                    multiply(b, n)

            loop(pool, first, pair, last)

        @block.scalar
        def _(act):
            act.wait_ge(weights_loaded, 16 * N_WEIGHT_LOADS)
            act.mul(qk_bias[:, 2, :], qk_bias[:, 0, :], SCALE).then_inc(scaled_bias, 1)
            act.wait_ge(scaled_bias, 1)
            b_done = Bb.emptied["act"]

            def a_features(ring, r, layer):
                for m in range(KT):
                    key = ("feat", layer, m)
                    ring.wait_filled(act, r, key)
                    nc.scalar.activation((feat_b, feat_a)[layer][:, m, :], bank_a(ring, key), ACT.Identity,
                                         bias=gb[:, 2 * layer + 1, m:m + 1],
                                         scale=gb[:, 2 * layer, m:m + 1]).then_inc(ring.emptied["act"], 1)

            def exp_adjacency(b, before):
                act.wait_ge(adj_max_ready, b.count(IT, IT))
                if before is not None:
                    act.wait_ge(probs_a_used, before.count(A_PROBS, NS))
                for it in range(IT):
                    nc.scalar.activation(exp_adj[:, it, :], adj_rows[:, it, :], ACT.Exp,
                                         bias=neg_adj_max[:, it:it + 1]).then_inc(exp_adj_ready, 1)

            def exp_adjacency_turned(ring, r, b):
                act.wait_ge(probs_a_ready, b.count(A_PROBS))
                for jt in range(IT):
                    ring.wait_filled(act, r, ("exp_t", jt))
                    nc.scalar.activation(exp_adj_t[:, jt, :], bank_a(ring, ("exp_t", jt)),
                                         ACT.Copy).then_inc(ring.emptied["act"], 1)

            def factor_rows(ring, r, b, layer):
                heads = H if layer == 0 else 1
                act.wait_ge(t_max_ready, b.count(2, layer + 1))
                bank = bank_a(ring, ("st", layer))
                nc.scalar.activation(fc_rows[64:64 + heads, :], bank[0:heads, :], ACT.Exp,
                                     bias=t_max[0:heads, 2:3], scale=1.0 - SLOPE)
                nc.scalar.activation(g_hl[64:64 + heads, :], bank[0:heads, :], ACT.Exp,
                                     bias=t_max[0:heads, 2:3], scale=1.0 - SLOPE).then_inc(exp_rows_ready, 1)
                nc.scalar.activation(fc_rows[0:heads, :], bank[32:32 + heads, :], ACT.Exp,
                                     bias=t_max[32:32 + heads, 1:2])
                nc.scalar.activation(fc_rows[32:32 + heads, :], bank[32:32 + heads, :], ACT.Exp,
                                     bias=t_max[32:32 + heads, 2:3], scale=-(1.0 - SLOPE)).then_inc(ring.emptied["act"], 1)

            def factor_columns(ring, r, layer):
                ring.wait_filled(act, r, ("cols", layer))
                nc.scalar.activation(fc_cols[:, layer, :, :],
                                     bank_a(ring, ("cols", layer)).rearrange("p (t c) -> p t c", c=P)[:, :, 0:64],
                                     ACT.Copy).then_inc(ring.emptied["act"], 1)

            def g_everywhere(ring, r, h):
                ring.wait_filled(act, r, ("g", h))
                nc.scalar.activation(g_all[:, h, :], bank_a(ring, ("g", h)), ACT.Copy).then_inc(ring.emptied["act"], 1)

            def g_everywhere_2(b):
                A.wait_filled(act, b, ("g2",))
                nc.scalar.activation(g_2[:], bank_a(A, ("g2",)), ACT.Copy).then_inc(A.emptied["act"], 1)

            def a_heads(b, q):
                act.wait_ge(probs_a_used, b.count(A_PROBS, (q + 1) * IT))
                last = q == QUADS - 1
                nc.scalar.activation(num_a[:, q, :], heads_a[:, 0, :], ACT.Copy).then_inc(heads_a_emptied, 1)
                if last:
                    nc.scalar.activation(den_a[:], heads_a[:, 1, :], ACT.Copy).then_inc(heads_a_emptied, 1)

            def keep_x3(b):
                act.wait_ge(out_ready, b.count(IT // 2))
                act.wait_ge(rows2_emptied, b.count(IT, IT))
                nc.scalar.activation(x3[:], x2[:], ACT.Copy).then_inc(x3_ready, 1)

            def adjacency_turned(b, multiplied):
                if multiplied is not None:
                    act.wait_ge(probs_b_vec, multiplied.count(len(DVE_STEPS), len(DVE_STEPS)))
                    act.wait_ge(probs_b_pool, multiplied.count(len(POOL_STEPS), len(POOL_STEPS)))
                for jt in range(IT):
                    A.wait_filled(act, b, ("adj_t", jt))
                    nc.scalar.activation(adj_t[:, jt, :], bank_a(A, ("adj_t", jt)), ACT.Copy,
                                         bias=ADJ_EPS).then_inc(A.emptied["act"], 1)

            def b_features(b):
                for m in range(KT):
                    Bb.wait_filled(act, b, ("feat", m))
                    nc.scalar.activation(feat_b[:, m, :], bank_b(("feat", m)), ACT.Copy).then_inc(b_done, 1)

            def q_or_k(b, name):
                high, bias, scale = (q_hi, 2, SCALE) if name == "q" else (k_hi, 1, 1.0)
                if name == "q":
                    act.wait_ge(stacks_loaded, b.count(16 * STACK_DMAS))
                    act.wait_ge(stored, b.count(16))
                else:
                    act.wait_ge(parts_split, b.count(2, 1))
                for m in range(KT):
                    Bb.wait_filled(act, b, (name, m))
                    nc.scalar.activation(qk_f32[:, m, :], bank_b((name, m)), ACT.Identity,
                                         bias=qk_bias[:, bias, m:m + 1], scale=scale)
                    nc.scalar.activation(high[:, m, :], bank_b((name, m)), ACT.Identity,
                                         bias=qk_bias[:, bias, m:m + 1], scale=scale).then_inc(b_done, 1)

            def gate_rows(b):
                Bb.wait_filled(act, b, ("ac",))
                nc.scalar.activation(ac_f32[:], bank_b(("ac",))[0:64, :], ACT.Identity, bias=bg[:])
                nc.scalar.activation(ac_hi, bank_b(("ac",))[0:64, :], ACT.Identity, bias=bg[:]).then_inc(b_done, 1)

            def maxima(b, q):
                act.wait_ge(max_loaded, b.count(16 * QUADS))
                Bb.wait_filled(act, b, ("max_t", q))
                nc.scalar.activation(max_t[:, q, :], bank_b(("max_t", q))[0:4, :], ACT.Copy).then_inc(b_done, 1)

            def exp_scores(b, n):
                if n >= B_BUFS:
                    act.wait_ge(probs_b_used, b.count(NS, n - B_BUFS + 1))
                else:
                    act.wait_ge(probs_b_used, b.count(NS))
                for g in range(4):
                    Bb.wait_filled(act, b, ("score", n, g))
                    nc.scalar.activation(probs_b[:, n % B_BUFS, g, :], bank_b(("score", n, g)),
                                         ACT.Exp).then_inc(b_done, 1)

            def b_heads(b, q):
                act.wait_ge(probs_b_used, b.count(NS, (q + 1) * IT))
                nc.scalar.activation(num_b[:, q, :], heads_b[:, 0, :], ACT.Copy).then_inc(heads_b_emptied, 1)
                if q == QUADS - 1:
                    nc.scalar.activation(den_b, heads_b[:, 1, :], ACT.Copy).then_inc(heads_b_emptied, 1)

            def front(ring, r, n, before):
                exp_adjacency(n, before)
                a_features(ring, r, 0)
                factor_rows(ring, r, n, 0)
                exp_adjacency_turned(ring, r, n)
                factor_columns(ring, r, 0)
                for h in range(H):
                    g_everywhere(ring, r, h)

            def b_front(b):
                b_features(b)
                q_or_k(b, "q")
                keep_x3(b)
                q_or_k(b, "k")
                gate_rows(b)

            def first(a, n):
                front(A0, a, a, None)
                a_heads(a, 0)
                a_heads(a, 1)
                a_features(A, a, 1)
                factor_rows(A, a, a, 1)
                factor_columns(A, a, 1)
                g_everywhere_2(a)
                front(A, a, n, a)
                a_heads(n, 0)
                adjacency_turned(a, None)

            def pair(n, a, b):
                b_front(b)
                a_heads(a, 1)
                exp_adjacency(n, a)
                a_features(A, a, 1)
                factor_rows(A, a, a, 1)
                factor_columns(A, a, 1)
                g_everywhere_2(a)
                a_features(A, a, 0)
                factor_rows(A, a, n, 0)
                exp_adjacency_turned(A, a, n)
                factor_columns(A, a, 0)
                for h in range(4):
                    g_everywhere(A, a, h)
                maxima(b, 0)
                exp_scores(b, 0)
                for h in range(4, H):
                    g_everywhere(A, a, h)
                exp_scores(b, 1)
                exp_scores(b, 2)
                maxima(b, 1)
                exp_scores(b, 3)
                exp_scores(b, 4)
                a_heads(n, 0)
                b_heads(b, 0)
                exp_scores(b, 5)
                exp_scores(b, 6)
                exp_scores(b, 7)
                b_heads(b, 1)
                adjacency_turned(a, b)

            def last(b):
                b_front(b)
                maxima(b, 0)
                for n in range(3):
                    exp_scores(b, n)
                maxima(b, 1)
                for n in range(3, 6):
                    exp_scores(b, n)
                b_heads(b, 0)
                exp_scores(b, 6)
                exp_scores(b, 7)
                b_heads(b, 1)

            loop(act, first, pair, last)

        @block.vector
        def _(dve):
            dve.wait_ge(consts_made, CONSTS)
            nc.vector.tensor_copy(select_head[:], select_f32).then_inc(rounded_consts, 1)
            nc.vector.memset(g_hl[:].bitcast(F32), 0.0)
            nc.vector.memset(wa1[:], 0.0)
            nc.vector.memset(wa2[:], 0.0).then_inc(vec_cleared, 1)
            dve.wait_ge(weights_loaded, 16 * N_WEIGHT_LOADS)
            dve.wait_ge(vec_cleared, 1)
            n = 0
            for layer, (w, wa, heads) in enumerate(((w1, wa1, H), (w2, wa2, 1))):
                for side in range(2):
                    for k in range(KT):
                        if n > 0:
                            dve.wait_ge(wa_ready, n)
                        nc.vector.tensor_tensor(wa_tmp, w[:, k, :], a_rows[:, 2 * layer + side, :],
                                                ALU.mult).then_inc(wa_products, 1)
                        dve.wait_ge(wa_products, n + 1)
                        nc.vector.tensor_reduce(wa[:, k, 32 * side:32 * side + heads],
                                                wa_tmp.rearrange("p (h d) -> p h d", h=heads),
                                                AX_X, ALU.add).then_inc(wa_ready, 1)
                        n += 1
            a_done, b_done = A.emptied["vec"], Bb.emptied["vec"]

            def layer_norm(b, layer):
                rows = x_rows if layer == 0 else x2
                if layer == 0:
                    dve.wait_ge(x_loaded, b.count(16, 16))
                for it in range(IT):
                    ins = nc.vector.bn_stats(stats[:, it, :], rows[:, it, :])
                ins.then_inc(stats_ready, 1)
                dve.wait_ge(stats_ready, b.count(2, layer + 1))
                nc.vector.memset(spare[:], 0.0)
                for it in range(IT):
                    ins = nc.vector.bn_aggr(mean_var[:, it, :], stats[:, it, :])
                ins.then_inc(mean_ready, 1)
                dve.wait_ge(mean_ready, b.count(2, layer + 1))
                nc.vector.tensor_scalar(var_eps[:, layer, :], mean_var[:, :, 1], LN_EPS, None,
                                        ALU.add).then_inc(var_ready, 1)

            def normalise(b, layer):
                rows, normal = ((x_rows, normed_1), (x2, normed))[layer]
                dve.wait_ge(rstd_ready, b.count(2, layer + 1))
                for it in range(IT):
                    nc.vector.tensor_scalar(normal[:, it, :], rows[:, it, :], mean_var[:, it, 0:1],
                                            rstd[:, layer, it:it + 1], ALU.subtract,
                                            ALU.mult).then_inc(normed_ready, 1)

            def adjacency_maxima(b, it):
                if it == 0:
                    dve.wait_ge(adj_loaded, b.count(16, 16))
                    dve.wait_ge(exp_adj_ready, b.count(IT))
                nc.vector.tensor_reduce(neg_adj_max[:, it:it + 1], adj_rows[:, it, :], AX_X, ALU.max,
                                        negate=True).then_inc(adj_max_ready, 1)

            def target_maximum(ring, r, b, layer):
                heads = H if layer == 0 else 1
                ring.wait_filled(dve, r, ("st", layer))
                nc.vector.tensor_reduce(t_max[32:32 + heads, 0:1], bank_a(ring, ("st", layer))[32:32 + heads, :],
                                        AX_X, ALU.max).then_inc(target_max_found, 1)
                dve.wait_ge(target_max_found, b.count(2, layer + 1))
                nc.vector.tensor_scalar(t_max[32:32 + heads, 1:2], t_max[32:32 + heads, 0:1], -1.0, None, ALU.mult)
                nc.vector.tensor_scalar(t_max[32:32 + heads, 2:3], t_max[32:32 + heads, 0:1], 1.0 - SLOPE, None,
                                        ALU.mult)
                nc.vector.tensor_scalar(t_max[0:heads, 2:3], t_max[32:32 + heads, 0:1], 1.0 - SLOPE, None,
                                        ALU.mult).then_inc(t_max_ready, 1)

            def g_low_part(b, layer):
                heads = H if layer == 0 else 1
                dve.wait_ge(exp_rows_ready, b.count(2, layer + 1))
                nc.vector.tensor_tensor(g_hl[96:96 + heads, :], fc_rows[64:64 + heads, :],
                                        g_hl[64:64 + heads, :].bitcast(F32), ALU.subtract).then_inc(g_split, 1)

            def values_1(ring, r):
                ring.wait_emptied(dve, r, ("cols", 0))
                c = fc_cols[:, 0, :, 0:H].unsqueeze(3)
                for q in range(QUADS):
                    hs = slice(4 * q, 4 * q + 4)
                    nc.vector.tensor_copy(c1[:, :, hs, q * HALF:(q + 1) * HALF],
                                          c[:, :, hs, :].broadcast_to((P, IT, 4, HALF)))
                for n in range(2):
                    ring.wait_filled(dve, r, ("h", 0, n))
                    nc.vector.tensor_tensor(v1[:, 2 * n:2 * n + 2, :, :], as_heads(as_rows(bank_a(ring, ("h", 0, n)))),
                                            c[:, 2 * n:2 * n + 2, :, :].broadcast_to((P, 2, H, DH)),
                                            ALU.mult).then_inc(ring.emptied["vec"], 1)

            def weights_1(ring, r, b, n):
                q, jt = STEPS[n]
                if jt == 0:
                    ring.wait_emptied(dve, r, ("g", 4 * q + 3))
                if n >= A_BUFS:
                    dve.wait_ge(probs_a_used, b.count(A_PROBS, n - A_BUFS + 1))
                elif n == 0:
                    dve.wait_ge(probs_a_used, b.count(A_PROBS))
                for g in range(4):
                    h = 4 * q + g
                    ins = nc.vector.scalar_tensor_tensor(
                        probs_a[:, n % A_BUFS, g, :], g_all[:, h, :], fc_cols[:, 0, jt, 32 + h:33 + h],
                        exp_adj_t[:, jt, :], ALU.max, ALU.mult)
                ins.then_inc(probs_a_ready, 1)

            def heads_reciprocal(ring, b, bank, recip, done):
                ring.wait_filled(dve, b, ("den",))
                nc.vector.reciprocal(recip[:].rearrange("p t q g -> p t g q"),
                                     bank.rearrange("p (t g q r) -> p t g q r", t=IT, g=4, q=QUADS)[:, :, :, :, 0]
                                     ).then_inc(done, 1)
                ring.wait_emptied(dve, b, ("den",))

            def normalised_rows(ring, b, n, bank, recip, into, done):
                ring.wait_filled(dve, b, ("back", n))
                nc.vector.tensor_tensor(as_heads(into[:, 2 * n:2 * n + 2, :]), as_heads(as_rows(bank)),
                                        recip[:, 2 * n:2 * n + 2, :, :].rearrange("p t q g -> p t (q g)").unsqueeze(3)
                                        .broadcast_to((P, 2, H, DH)), ALU.mult).then_inc(done, 1)

            def first_layer_rows(b):
                heads_reciprocal(A, b, bank_a(A, ("den",)), recip_a, a_done)
                dve.wait_ge(x3_ready, b.count(1))
                for n in range(2):
                    rows = slice(2 * n, 2 * n + 2)
                    normalised_rows(A, b, n, bank_a(A, ("back", n)), recip_a, x2, a_done)
                    A.wait_emptied(dve, b, ("back", n))
                    nc.vector.tensor_tensor(x2[:, rows, :], x2[:, rows, :], x_rows[:, rows, :],
                                            ALU.add).then_inc(x2_ready, 1)
                dve.wait_ge(x2_ready, b.count(IT // 2, IT // 2))

            def values_2(b):
                A.wait_emptied(dve, b, ("cols", 1))
                A.wait_emptied(dve, b, ("h", 1, 1))
                nc.vector.tensor_copy(v2[:, :, D:D + 2], fc_cols[:, 1, :, 0:1].broadcast_to((P, IT, 2)))
                nc.vector.tensor_tensor(v2[:, :, 0:D], v2[:, :, 0:D],
                                        fc_cols[:, 1, :, 0:1].broadcast_to((P, IT, D)), ALU.mult)

            def raw_values_2(b):
                for n in range(2):
                    A.wait_filled(dve, b, ("h", 1, n))
                    nc.vector.tensor_copy(v2[:, 2 * n:2 * n + 2, 0:D],
                                          as_rows(bank_a(A, ("h", 1, n)))).then_inc(a_done, 1)

            def weights_2(b):
                A.wait_emptied(dve, b, ("g2",))
                dve.wait_ge(probs_a_used, b.count(A_PROBS, NS))
                for jt in range(IT):
                    ins = nc.vector.scalar_tensor_tensor(
                        probs_a[:, NS % A_BUFS, jt, :], g_2[:], fc_cols[:, 1, jt, 32:33],
                        exp_adj_t[:, jt, :], ALU.max, ALU.mult)
                ins.then_inc(probs_a_ready, 1)

            def second_layer_rows(b, it):
                if it < IT - 1:
                    dve.wait_ge(rows2_filled, b.count(IT - 1, it + 1))
                else:
                    dve.wait_ge(probs_a_used, b.count(A_PROBS, A_PROBS))
                nc.vector.reciprocal(recip_2[:, it:it + 1], heads_a[:, it % 2, D:D + 1]).then_inc(recip_2_ready, 1)
                dve.wait_ge(recip_2_ready, b.count(IT, it + 1))
                nc.vector.scalar_tensor_tensor(x2[:, it, :], heads_a[:, it % 2, 0:D], recip_2[:, it:it + 1],
                                               x2[:, it, :], ALU.mult, ALU.add).then_inc(rows2_emptied, 1)

            def low_parts(b, name, high, low):
                for m in range(KT):
                    Bb.wait_emptied(dve, b, (name, m))
                    ins = nc.vector.tensor_tensor(low[:, m, :], qk_f32[:, m, :], high[:, m, :].bitcast(F32),
                                                  ALU.subtract)
                return ins

            def split_q(b):
                low_parts(b, "q", q_hi, q_lo).then_inc(parts_split, 1)

            def split_k_and_gates(b):
                low_parts(b, "k", k_hi, k_lo)
                Bb.wait_emptied(dve, b, ("ac",))
                nc.vector.tensor_tensor(ac_lo, ac_f32[:], ac_hi.bitcast(F32),
                                        ALU.subtract).then_inc(parts_split, 1)

            def values_3(b):
                for n in range(2):
                    Bb.wait_filled(dve, b, ("v", n))
                    nc.vector.tensor_tensor(v3[:, 2 * n:2 * n + 2, :], as_rows(bank_b(("v", n))),
                                            bv[:].unsqueeze(1).broadcast_to((P, 2, D)), ALU.add).then_inc(b_done, 1)

            def maxima(b, h, tiles=range(IT)):
                for it in tiles:
                    Bb.wait_filled(dve, b, ("max", h, it))
                    nc.vector.tensor_reduce(row_max[:, it, h:h + 1], bank_b(("max", h, it)),
                                            AX_X, ALU.max).then_inc(b_done, 1)

            def multiply(b, n):
                Bb.wait_emptied(dve, b, ("score", n, 3))
                p = probs_b[:, n % B_BUFS, :, :]
                jt = STEPS[n][1]
                nc.vector.tensor_tensor(p, p, adj_t[:, jt:jt + 1, :].broadcast_to((P, 4, N)),
                                        ALU.mult).then_inc(probs_b_vec, 1)

            def attention_rows(b):
                heads_reciprocal(Bb, b, bank_b(("den",)), recip_b, b_done)
                for n in range(2):
                    rows = slice(2 * n, 2 * n + 2)
                    normalised_rows(Bb, b, n, bank_b(("back", n)), recip_b, out_rows, b_done)
                    Bb.wait_emptied(dve, b, ("back", n))
                    nc.vector.tensor_tensor(out_rows[:, rows, :], out_rows[:, rows, :], x3[:, rows, :],
                                            ALU.add).then_inc(out_ready, 1)

            def first(a, n):
                for it in range(IT):
                    adjacency_maxima(a, it)
                layer_norm(a, 0)
                normalise(a, 0)
                target_maximum(A0, a, a, 0)
                g_low_part(a, 0)
                values_1(A0, a)
                for s in range(NS):
                    weights_1(A0, a, a, s)
                first_layer_rows(a)
                layer_norm(a, 1)
                for it in range(IT):
                    adjacency_maxima(n, it)
                normalise(a, 1)
                target_maximum(A, a, a, 1)
                g_low_part(a, 1)
                raw_values_2(a)
                values_2(a)
                weights_2(a)
                layer_norm(n, 0)
                normalise(n, 0)
                target_maximum(A, a, n, 0)
                g_low_part(n, 0)
                for it in range(IT):
                    second_layer_rows(a, it)
                values_1(A, a)
                for s in range(AHEAD):
                    weights_1(A, a, n, s)

            def pair(n, a, b):
                def weights(s):
                    weights_1(A, b, a, s)

                weights(6)
                split_q(b)
                weights(7)
                split_k_and_gates(b)
                for it in range(IT):
                    adjacency_maxima(n, it)
                first_layer_rows(a)
                values_3(b)
                layer_norm(a, 1)
                maxima(b, 0, (0, 1))
                normalise(a, 1)
                layer_norm(n, 0)
                maxima(b, 0, (2, 3))
                normalise(n, 0)
                target_maximum(A, a, a, 1)
                maxima(b, 1, (0, 1))
                g_low_part(a, 1)
                raw_values_2(a)
                values_2(a)
                weights_2(a)
                maxima(b, 1, (2, 3))
                target_maximum(A, a, n, 0)
                second_layer_rows(a, 0)
                g_low_part(n, 0)
                maxima(b, 2, (0, 1))
                second_layer_rows(a, 1)
                maxima(b, 2, (2, 3))
                second_layer_rows(a, 2)
                maxima(b, 3, (0, 1))
                second_layer_rows(a, 3)
                maxima(b, 3, (2, 3))
                maxima(b, 4)
                values_1(A, a)
                weights_1(A, a, n, 0)
                maxima(b, 5)
                weights_1(A, a, n, 1)
                maxima(b, 6)
                weights_1(A, a, n, 2)
                maxima(b, 7)
                weights_1(A, a, n, 3)
                multiply(b, 4)
                weights_1(A, a, n, 4)
                multiply(b, 6)
                weights_1(A, a, n, 5)
                multiply(b, 7)
                attention_rows(b)

            def last(b):
                split_q(b)
                split_k_and_gates(b)
                values_3(b)
                for h in range(H):
                    maxima(b, h)
                for n in DVE_STEPS:
                    multiply(b, n)
                attention_rows(b)

            loop(dve, first, pair, last)

        @block.tensor
        def _(pe):
            pe.wait_ge(consts_made, CONSTS)
            pe.wait_ge(rounded_consts, 1)
            pe.wait_ge(wa_ready, 8)
            pe.wait_ge(stack_consts, 16 * (2 + N // P))

            def turn(bank, rows, m, it):
                return nc.tensor.transpose(bank[:, it * P:(it + 1) * P], rows[:, it, m * P:(m + 1) * P], ident[:])

            def a_features(ring, r, b, layer):
                for m in range(KT):
                    ring.wait_free(pe, r, ("feat", layer, m))
                    for it in range(IT):
                        if m == 0:
                            pe.wait_ge(normed_ready, b.count(2 * IT, layer * IT + it + 1))
                        mm = turn(bank_a(ring, ("feat", layer, m)), (normed_1, normed)[layer], m, it)
                    mm.then_inc(ring.filled, 1)

            def source_and_target(ring, r, layer):
                ring.wait_free(pe, r, ("st", layer))
                wa = wa1 if layer == 0 else wa2
                for k in range(KT):
                    ring.wait_emptied(pe, r, ("feat", layer, k))
                    mm = nc.tensor.matmul(bank_a(ring, ("st", layer))[0:64, :], wa[:, k, :],
                                          (feat_b, feat_a)[layer][:, k, :],
                                          start=(k == 0), stop=(k == KT - 1))
                mm.then_inc(ring.filled, 1)

            def turn_exp_adjacency(ring, r, b):
                for jt in range(IT):
                    ring.wait_free(pe, r, ("exp_t", jt))
                    for it in range(IT):
                        if jt == 0:
                            pe.wait_ge(exp_adj_ready, b.count(IT, it + 1))
                        mm = turn(bank_a(ring, ("exp_t", jt)), exp_adj, jt, it)
                    mm.then_inc(ring.filled, 1)

            def factor_columns(ring, r, layer):
                ring.wait_free(pe, r, ("cols", layer))
                ring.wait_emptied(pe, r, ("st", layer))
                for jt in range(IT):
                    mm = nc.tensor.transpose(bank_a(ring, ("cols", layer))[:, P * jt:P * jt + P],
                                             fc_rows[:, jt * P:(jt + 1) * P], ident[:])
                mm.then_inc(ring.filled, 1)

            def rows_times(ring, r, key, bank, features, w, n):
                ring.wait_free(pe, r, key)
                for t in range(2):
                    for k in range(KT):
                        it = 2 * n + t
                        mm = nc.tensor.matmul(as_rows(bank)[:, t, :], features[:, k, it * P:(it + 1) * P],
                                              w[:, k, :], start=(k == 0), stop=(k == KT - 1))
                mm.then_inc(ring.filled, 1)

            def values_1(ring, r, halves=(0, 1)):
                for n in halves:
                    rows_times(ring, r, ("h", 0, n), bank_a(ring, ("h", 0, n)), feat_b, w1, n)

            def values_2(b):
                for n in range(2):
                    rows_times(A, b, ("h", 1, n), bank_a(A, ("h", 1, n)), feat_a, w2, n)

            def g_everywhere(ring, r, b, h):
                ring.wait_free(pe, r, ("g", h))
                if h == 0:
                    pe.wait_ge(g_split, b.count(2, 1))
                nc.tensor.matmul(bank_a(ring, ("g", h)), select_head[:, h, :], g_hl[:], start=True,
                                 stop=True).then_inc(ring.filled, 1)

            def g_everywhere_2(b):
                A.wait_free(pe, b, ("g2",))
                pe.wait_ge(g_split, b.count(2, 2))
                nc.tensor.matmul(bank_a(A, ("g2",)), select_head[:, 0, :], g_hl[:], start=True,
                                 stop=True).then_inc(A.filled, 1)

            def four_heads(banks, probs, n, which, stationary):
                q, jt = STEPS[n]
                for g in range(4):
                    mm = nc.tensor.matmul(
                        banks[32 * g:32 * g + 32, which, :], stationary(q, jt, 4 * q + g), probs[:, g, :],
                        start=(n == 0 if which else jt == 0), stop=(n == NS - 1 if which else jt == IT - 1),
                        tile_position=(0, 32 * g))
                return mm

            def a_numerators(ring, r, b, n):
                pe.wait_ge(probs_a_ready, b.count(A_PROBS, n + 1))
                if n == 0:
                    pe.wait_ge(rows2_emptied, b.count(IT))
                    ring.wait_emptied(pe, r, ("h", 0, 1))
                if n == IT:
                    pe.wait_ge(heads_a_emptied, b.count(QUADS + 1, 1))
                four_heads(heads_a, probs_a[:, n % A_BUFS, :, :], n, 0, lambda q, jt, h: v1[:, jt, h, :])

            def a_denominators(n):
                four_heads(heads_a, probs_a[:, n % A_BUFS, :, :], n, 1,
                           lambda q, jt, h: c1[:, jt, h, :]).then_inc(probs_a_used, 1)

            def a_step(ring, r, b, n):
                a_numerators(ring, r, b, n)
                a_denominators(n)

            def turn_back(ring, b, bank_of, numerators, denominators):
                ring.wait_free(pe, b, ("den",))
                for it in range(IT):
                    mm = nc.tensor.transpose(bank_of(("den",))[:, it * P:(it + 1) * P],
                                             denominators[:, it * P:(it + 1) * P], ident[:])
                mm.then_inc(ring.filled, 1)
                for n in range(2):
                    ring.wait_free(pe, b, ("back", n))
                    for t in range(2):
                        for q in range(QUADS):
                            it = 2 * n + t
                            mm = nc.tensor.transpose(as_rows(bank_of(("back", n)))[:, t, q * P:(q + 1) * P],
                                                     numerators[:, q, it * P:(it + 1) * P], ident[:])
                    mm.then_inc(ring.filled, 1)

            def a_back(b):
                pe.wait_ge(heads_a_emptied, b.count(QUADS + 1, QUADS + 1))
                turn_back(A, b, lambda key: bank_a(A, key), num_a, den_a)

            def second_layer(b, tiles=range(IT)):
                if 0 in tiles:
                    pe.wait_ge(probs_a_ready, b.count(A_PROBS, A_PROBS))
                for it in tiles:
                    if it >= 2:
                        pe.wait_ge(rows2_emptied, b.count(IT, it - 1))
                    for jt in range(IT):
                        mm = nc.tensor.matmul(heads_a[:, it % 2, 0:D + 2],
                                              probs_a[:, NS % A_BUFS, jt, it * P:(it + 1) * P],
                                              v2[:, jt, :], start=(jt == 0), stop=(jt == IT - 1))
                    mm.then_inc(rows2_filled if it < IT - 1 else probs_a_used, 1)

            def turn_adjacency(b):
                pe.wait_ge(adj_loaded_again, b.count(16, 16))
                for jt in range(IT):
                    A.wait_free(pe, b, ("adj_t", jt))
                    for it in range(IT):
                        mm = turn(bank_a(A, ("adj_t", jt)), adj_rows, jt, it)
                    mm.then_inc(A.filled, 1)

            def b_features(b):
                for m in range(KT):
                    Bb.wait_free(pe, b, ("feat", m))
                    for it in range(IT):
                        if m == 0:
                            pe.wait_ge(rows2_emptied, b.count(IT, it + 1))
                        mm = turn(bank_b(("feat", m)), x2, m, it)
                    mm.then_inc(Bb.filled, 1)

            def queries_or_keys(b, name, w):
                if name == "q":
                    for k in range(KT):
                        Bb.wait_emptied(pe, b, ("feat", k))
                for m in range(KT):
                    Bb.wait_free(pe, b, (name, m))
                    for k in range(KT):
                        mm = nc.tensor.matmul(bank_b((name, m)), w[:, k, m * P:(m + 1) * P],
                                              feat_b[:, k, :], start=(k == 0), stop=(k == KT - 1))
                    mm.then_inc(Bb.filled, 1)

            def gates(b):
                Bb.wait_free(pe, b, ("ac",))
                for k in range(KT):
                    mm = nc.tensor.matmul(bank_b(("ac",))[0:64, :], wg[:, k, :], feat_b[:, k, :],
                                          start=(k == 0), stop=(k == KT - 1))
                mm.then_inc(Bb.filled, 1)

            def values_3(b):
                for n in range(2):
                    rows_times(Bb, b, ("v", n), bank_b(("v", n)), feat_b, wv, n)

            def maxima(b, h, tiles=range(IT)):
                if h == 0 and 0 in tiles:
                    pe.wait_ge(stacks_loaded, b.count(16 * STACK_DMAS, 16 * STACK_DMAS))
                for it in tiles:
                    Bb.wait_free(pe, b, ("max", h, it))
                    nc.tensor.matmul(bank_b(("max", h, it)), q_stack[0:104, h, it * P:(it + 1) * P],
                                     k_stack[0:104, h, :], start=True, stop=True).then_inc(Bb.filled, 1)

            def turn_maxima(b, q):
                Bb.wait_emptied(pe, b, ("max", 4 * q + 3, IT - 1))
                Bb.wait_free(pe, b, ("max_t", q))
                for it in range(IT):
                    mm = nc.tensor.transpose(bank_b(("max_t", q))[0:4, it * P:(it + 1) * P],
                                             row_max[:, it, 4 * q:4 * q + 4], ident[:])
                mm.then_inc(Bb.filled, 1)

            def scores(b, n, heads=range(4)):
                q, jt = STEPS[n]
                if jt == 0 and 0 in heads:
                    pe.wait_ge(max_loaded, b.count(16 * QUADS, 16 * q + 16))
                for g in heads:
                    Bb.wait_free(pe, b, ("score", n, g))
                    nc.tensor.matmul(bank_b(("score", n, g)), k_stack[:, 4 * q + g, jt * P:(jt + 1) * P],
                                     q_stack[:, 4 * q + g, :], start=True, stop=True).then_inc(Bb.filled, 1)

            def b_numerators(b, n):
                if n == 0:
                    pe.wait_ge(heads_b_emptied, b.count(QUADS + 1))
                    Bb.wait_emptied(pe, b, ("v", 1))
                if n == IT:
                    pe.wait_ge(heads_b_emptied, b.count(QUADS + 1, 1))
                if n in DVE_STEPS:
                    pe.wait_ge(probs_b_vec, b.count(len(DVE_STEPS), DVE_STEPS.index(n) + 1))
                else:
                    pe.wait_ge(probs_b_pool, b.count(len(POOL_STEPS), POOL_STEPS.index(n) + 1))
                four_heads(heads_b, probs_b[:, n % B_BUFS, :, :], n, 0,
                           lambda q, jt, h: v3[:, jt, h * DH:(h + 1) * DH])

            def b_denominators(n):
                four_heads(heads_b, probs_b[:, n % B_BUFS, :, :], n, 1,
                           lambda q, jt, h: ones[:, q, :]).then_inc(probs_b_used, 1)

            def b_step(b, n):
                b_numerators(b, n)
                b_denominators(n)

            def b_back(b):
                pe.wait_ge(heads_b_emptied, b.count(QUADS + 1, QUADS + 1))
                turn_back(Bb, b, bank_b, num_b, den_b)

            def front(ring, r, n):
                a_features(ring, r, n, 0)
                source_and_target(ring, r, 0)
                turn_exp_adjacency(ring, r, n)
                factor_columns(ring, r, 0)
                for h in range(4):
                    g_everywhere(ring, r, n, h)
                values_1(ring, r)
                for h in range(4, H):
                    g_everywhere(ring, r, n, h)

            def first(a, n):
                front(A0, a, a)
                A0.wait_emptied(pe, a, ("g", H - 1))
                for s in range(NS):
                    a_step(A0, a, a, s)
                a_back(a)
                a_features(A, a, a, 1)
                source_and_target(A, a, 1)
                values_2(a)
                factor_columns(A, a, 1)
                g_everywhere_2(a)
                a_features(A, a, n, 0)
                source_and_target(A, a, 0)
                turn_exp_adjacency(A, a, n)
                second_layer(a)
                factor_columns(A, a, 0)
                for h in range(4):
                    g_everywhere(A, a, n, h)
                values_1(A, a)
                for h in range(4, H):
                    g_everywhere(A, a, n, h)
                for s in range(AHEAD):
                    a_step(A, a, n, s)
                turn_adjacency(a)

            def pair(n, a, b):
                b_features(b)
                queries_or_keys(b, "q", wq)
                a_step(A, b, a, 6)
                queries_or_keys(b, "k", wk)
                a_step(A, b, a, 7)
                gates(b)
                a_back(a)
                values_3(b)
                maxima(b, 0, (0, 1))
                a_features(A, a, a, 1)
                maxima(b, 0, (2, 3))
                source_and_target(A, a, 1)
                maxima(b, 1, (0, 1))
                values_2(a)
                factor_columns(A, a, 1)
                g_everywhere_2(a)
                a_features(A, a, n, 0)
                maxima(b, 1, (2, 3))
                source_and_target(A, a, 0)
                second_layer(a, (0,))
                maxima(b, 2, (0, 1))
                second_layer(a, (1,))
                turn_exp_adjacency(A, a, n)
                maxima(b, 2, (2, 3))
                second_layer(a, (2,))
                factor_columns(A, a, 0)
                maxima(b, 3, (0, 1))
                second_layer(a, (3,))
                g_everywhere(A, a, n, 0)
                g_everywhere(A, a, n, 1)
                maxima(b, 3, (2, 3))
                g_everywhere(A, a, n, 2)
                g_everywhere(A, a, n, 3)
                turn_maxima(b, 0)
                values_1(A, a, (0,))
                maxima(b, 4, (0, 1))
                values_1(A, a, (1,))
                maxima(b, 4, (2, 3))
                scores(b, 0, (0, 1))
                g_everywhere(A, a, n, 4)
                g_everywhere(A, a, n, 5)
                scores(b, 0, (2, 3))
                g_everywhere(A, a, n, 6)
                g_everywhere(A, a, n, 7)
                maxima(b, 5)
                scores(b, 1, (0, 1))
                a_numerators(A, a, n, 0)
                scores(b, 1, (2, 3))
                a_denominators(0)
                maxima(b, 6, (0, 1))
                b_numerators(b, 0)
                maxima(b, 6, (2, 3))
                b_denominators(0)
                scores(b, 2, (0, 1))
                a_numerators(A, a, n, 1)
                scores(b, 2, (2, 3))
                a_denominators(1)
                maxima(b, 7, (0, 1))
                b_numerators(b, 1)
                maxima(b, 7, (2, 3))
                b_denominators(1)
                turn_maxima(b, 1)
                scores(b, 3, (0, 1))
                a_numerators(A, a, n, 2)
                scores(b, 3, (2, 3))
                a_denominators(2)
                b_step(b, 2)
                scores(b, 4, (0, 1))
                a_numerators(A, a, n, 3)
                scores(b, 4, (2, 3))
                a_denominators(3)
                b_step(b, 3)
                scores(b, 5, (0, 1))
                b_numerators(b, 4)
                scores(b, 5, (2, 3))
                b_denominators(4)
                scores(b, 6, (0, 1))
                a_numerators(A, a, n, 4)
                scores(b, 6, (2, 3))
                a_denominators(4)
                b_step(b, 5)
                scores(b, 7, (0, 1))
                a_numerators(A, a, n, 5)
                scores(b, 7, (2, 3))
                a_denominators(5)
                b_step(b, 6)
                b_step(b, 7)
                turn_adjacency(a)
                b_back(b)

            def last(b):
                b_features(b)
                queries_or_keys(b, "q", wq)
                queries_or_keys(b, "k", wk)
                gates(b)
                values_3(b)
                for h in range(4):
                    maxima(b, h)
                turn_maxima(b, 0)
                maxima(b, 4)
                scores(b, 0)
                maxima(b, 5)
                scores(b, 1)
                maxima(b, 6)
                scores(b, 2)
                b_step(b, 0)
                maxima(b, 7)
                turn_maxima(b, 1)
                for n in range(3, NS + 2):
                    if n < NS:
                        scores(b, n)
                    b_step(b, n - 2)
                b_back(b)

            loop(pe, first, pair, last)


_INS = ["x", "adj", "L0_gnn_W1", "L0_gnn_a_src1", "L0_gnn_a_dst1", "L0_gnn_g1", "L0_gnn_b1", "L0_gnn_W2",
        "L0_gnn_a_src2", "L0_gnn_a_dst2", "L0_gnn_g2", "L0_gnn_b2", "L1_gnn_W_q", "L1_gnn_b_q", "L1_gnn_W_k",
        "L1_gnn_b_k", "L1_gnn_W_v", "L1_gnn_b_v", "L1_gnn_w_g", "L1_gnn_b_g"]


def kernel(**inputs):
    import numpy as _np
    import concourse.bacc as _bacc
    from concourse import mybir as _mybir
    from concourse.bass_utils import run_bass_kernel_spmd as _run

    nc = _bacc.Bacc("TRN2", target_bir_lowering=False, num_devices=1)
    arrays, args = {}, []
    for name in _INS:
        a = _np.ascontiguousarray(inputs[name])
        if a.ndim == 0:
            a = a.reshape(1)
        arrays[f"in_{name}_dram"] = a
        args.append(nc.dram_tensor(f"in_{name}_dram", a.shape, _mybir.dt.from_np(a.dtype), kind="ExternalInput").ap())
    shape = inputs["x"].shape
    args.append(nc.dram_tensor("out_0_dram", shape, _mybir.dt.float32, kind="ExternalOutput").ap())
    two_gat_layers_then_biased_attention(nc, *args)
    r = _run(nc, [arrays], core_ids=[0])
    return r.results[0]["out_0_dram"]
```

```python
from contextlib import ExitStack

import concourse.bass as bass
from concourse import mybir

F32 = mybir.dt.float32
F32R = mybir.dt.float32r
ALU = mybir.AluOpType
ACT = mybir.ActivationFunctionType
AX_X = mybir.AxisListType.X

P = 128
START = 3


class Batch:

    def __init__(self, register, shift=0):
        self.register, self.shift = register, shift

    def count(self, per_batch, more=0):
        return self.register * per_batch + (self.shift * per_batch + more + START)


class Banks:

    def __init__(self, fills, size, filled, emptied):
        self.fills, self.size, self.filled, self.emptied = fills, size, filled, emptied
        self.number = {key: n for n, (key, _) in enumerate(fills)}
        self.by = {key: engine for key, engine in fills}
        self.total = {e: sum(engine == e for _, engine in fills) for e in emptied}

    def bank(self, key):
        return self.number[key] % self.size

    def fill_count(self, b, key):
        return b.count(len(self.fills), self.number[key] + 1)

    def empty_count(self, b, key):
        e = self.by[key]
        return b.count(self.total[e], sum(engine == e for _, engine in self.fills[:self.number[key] + 1]))

    def wait_filled(self, eng, b, key):
        eng.wait_ge(self.filled, self.fill_count(b, key))

    def wait_emptied(self, eng, b, key):
        eng.wait_ge(self.emptied[self.by[key]], self.empty_count(b, key))

    def wait_free(self, pe, b, key):
        n = self.number[key] - self.size
        if n >= 0:
            self.wait_emptied(pe, b, self.fills[n][0])
        else:
            last = max(m for m in range(len(self.fills)) if m % self.size == self.bank(key))
            later = [engine for _, engine in self.fills[last:]]
            pe.wait_ge(self.emptied[later[0]], b.count(self.total[later[0]], 1 - later.count(later[0])))


def two_gat_layers_then_biased_attention(
    nc, x, adj, W1, a_src1, a_dst1, g1, b1, W2, a_src2, a_dst2, g2, b2,
    W_q, b_q, W_k, b_k, W_v, b_v, w_g, b_g, out,
):
    B, N, D = x.shape
    H, DH = a_src1.shape
    IT = N // P
    KT = D // P
    QUADS = H // 4
    HALF = DH // QUADS
    SCALE = float(DH) ** -0.5
    LN_EPS = 1e-6
    ADJ_EPS = 1e-9
    SLOPE = 0.2
    A_BUFS, B_BUFS = 2, 3
    assert DH == 32 and D == 256 and N == 512 and KT == QUADS == 2

    STEPS = [(q, jt) for q in range(QUADS) for jt in range(IT)]
    NS = len(STEPS)
    DVE_STEPS = [4, 5, 7]
    POOL_STEPS = [n for n in range(NS) if n not in DVE_STEPS]
    A_PROBS = NS + 1

    with ExitStack() as ctx:
        def sb(name, shape, dt=F32):
            return ctx.enter_context(nc.sbuf_tensor(name, shape, dt))

        def ps(name, shape):
            return ctx.enter_context(nc.psum_tensor(name, shape, F32))

        ident = sb("ident", [P, P])
        select_head = sb("select_head", [P, H, P], F32R)
        ones = sb("ones", [P, QUADS, DH])
        minus_half = sb("minus_half", [P, IT])
        w1 = sb("w1", [P, KT, D])
        w2 = sb("w2", [P, KT, D])
        wq = sb("wq", [P, KT, D])
        wk = sb("wk", [P, KT, D])
        wv = sb("wv", [P, KT, D])
        wg = sb("wg", [P, KT, 64])
        wa1 = sb("wa1", [P, KT, 64])
        wa2 = sb("wa2", [P, KT, 64])
        gb = sb("gb", [P, 4, KT])
        qk_bias = sb("qk_bias", [P, 3, KT])
        bv = sb("bv", [P, D])
        bg = sb("bg", [64, 1])

        x_rows = sb("x_rows", [P, IT, D])
        adj_rows = sb("adj_rows", [P, IT, N])
        neg_adj_max = sb("neg_adj_max", [P, IT])
        exp_adj_t = sb("exp_adj_t", [P, IT, N])
        stats = sb("stats", [P, IT, 6])
        mean_var = sb("mean_var", [P, IT, 2])
        var_eps = sb("var_eps", [P, 2, IT])
        rstd = sb("rstd", [P, 2, IT])
        spare = sb("spare", [P, 1])
        normed = sb("normed", [P, IT, D])
        feat_a = sb("feat_a", [P, KT, N])
        t_max = sb("t_max", [64, 4])
        g_hl = sb("g_hl", [P, N], F32R)
        fc_rows = sb("fc_rows", [P, N])
        fc_cols = sb("fc_cols", [P, 2, IT, 64])
        g_all = sb("g_all", [P, H, N])
        v1 = sb("v1", [P, IT, H, DH])
        c1 = sb("c1", [P, IT, H, DH])
        v2 = sb("v2", [P, IT, D + 2])
        probs_a = sb("probs_a", [P, A_BUFS, 4, N])
        exp_adj = probs_a[:, 1, :, :]
        num_a = normed[:].rearrange("p (q r) d -> p q (r d)", q=QUADS)
        den_a = sb("den_a", [P, N])
        g_2 = den_a
        recip_a = sb("recip_a", [P, IT, QUADS, 4])
        recip_2 = sb("recip_2", [P, IT])
        x2 = sb("x2", [P, IT, D])

        adj_t = sb("adj_t", [P, IT, N])
        x3 = sb("x3", [P, IT, D])

        feat_b = sb("feat_b", [P, KT, N])
        v3 = sb("v3", [P, IT, D])
        qk_f32 = sb("qk_f32", [P, KT, N])
        out_rows = qk_f32[:].rearrange("p k (c d) -> p (k c) d", d=D)
        normed_1 = out_rows
        q_hi = sb("q_hi", [P, KT, N], F32R)
        q_lo = sb("q_lo", [P, KT, N], F32R)
        k_hi = sb("k_hi", [P, KT, N], F32R)
        k_lo = sb("k_lo", [P, KT, N], F32R)
        ac_f32 = sb("ac_f32", [64, N])
        ac_parts = sb("ac_parts", [P, N], F32R)
        ac_hi, ac_lo = ac_parts[0:64, :], ac_parts[64:P, :]
        row_max = sb("row_max", [P, IT, H])
        max_t = sb("max_t", [4, QUADS, N], F32R)
        q_stack = sb("q_stack", [P, H, N], F32R)
        k_stack = sb("k_stack", [P, H, N], F32R)
        probs_b = sb("probs_b", [P, B_BUFS, 4, N])
        num_b = q_hi[:].bitcast(F32)
        den_b = q_lo[:, 0, :].bitcast(F32)
        recip_b = sb("recip_b", [P, IT, QUADS, 4])

        select_f32 = probs_b[:, 0, 0:2, :].rearrange("p a (c n) -> p (a c) n", n=P)
        a_rows = probs_b[:, 0, 2:4, :].rearrange("p a (c n) -> p (a c) n", n=D)
        minus_head_f32 = probs_b[0:H, 1, 0:2, :].rearrange("p a (c n) -> p (a c) n", n=P)
        minus_head = probs_b[0:H, 1, 2:4, :].rearrange("p a (c n) -> p (a c) n", n=P)
        ones_row = probs_b[0:2, 2, 0, :]
        wa_tmp = probs_b[:, 2, 2, 0:D]

        heads_a = ps("heads_a", [P, 2, N])
        heads_b = ps("heads_b", [P, 2, N])
        ring_a = ps("ring_a", [P, 2, N])
        ring_b = ps("ring_b", [P, 2, N])

        def sem(name):
            return ctx.enter_context(nc.semaphore(name))

        weights_loaded = sem("weights_loaded")
        consts_made = sem("consts_made")
        rounded_consts = sem("rounded_consts")
        stack_consts = sem("stack_consts")
        wa_products = sem("wa_products")
        wa_ready = sem("wa_ready")
        vec_cleared = sem("vec_cleared")
        scaled_bias = sem("scaled_bias")

        loop_sems = []

        def counted(name):
            loop_sems.append(sem(name))
            return loop_sems[-1]

        x_loaded = counted("x_loaded")
        adj_loaded = counted("adj_loaded")
        adj_loaded_again = counted("adj_loaded_again")
        strip_loaded = [counted(f"strip_loaded_{g}") for g in range(4)]
        gates_loaded = counted("gates_loaded")
        max_loaded = counted("max_loaded")
        stored = counted("stored")
        adj_max_ready = counted("adj_max_ready")
        exp_adj_ready = counted("exp_adj_ready")
        var_ready = counted("var_ready")
        rstd_ready = counted("rstd_ready")
        normed_ready = counted("normed_ready")
        t_max_ready = counted("t_max_ready")
        exp_rows_ready = counted("exp_rows_ready")
        g_split = counted("g_split")
        probs_a_ready = counted("probs_a_ready")
        probs_a_used = counted("probs_a_used")
        rows2_filled = counted("rows2_filled")
        rows2_emptied = counted("rows2_emptied")
        heads_a_emptied = counted("heads_a_emptied")
        x2_ready = counted("x2_ready")
        x3_ready = counted("x3_ready")
        parts_split = counted("parts_split")
        probs_b_vec = counted("probs_b_vec")
        probs_b_pool = counted("probs_b_pool")
        probs_b_used = counted("probs_b_used")
        heads_b_emptied = counted("heads_b_emptied")
        out_ready = counted("out_ready")
        stats_ready = counted("stats_ready")
        mean_ready = counted("mean_ready")
        target_max_found = counted("target_max_found")
        recip_2_ready = counted("recip_2_ready")

        front_fills = [(("feat", 0, m), "act") for m in range(KT)] + [(("st", 0), "act")] \
            + [(("exp_t", jt), "act") for jt in range(IT)] + [(("cols", 0), "act")] \
            + [(("g", h), "act") for h in range(4)] + [(("h", 0, n), "vec") for n in range(2)] \
            + [(("g", h), "act") for h in range(4, H)]
        A = Banks(
            [(("den",), "vec")] + [(("back", n), "vec") for n in range(2)]
            + [(("feat", 1, m), "act") for m in range(KT)] + [(("st", 1), "act")]
            + [(("cols", 1), "act"), (("g2",), "act")] + [(("h", 1, n), "act") for n in range(2)]
            + front_fills + [(("adj_t", jt), "act") for jt in range(IT)],
            2, counted("a_filled"), {"act": counted("a_emptied_act"), "vec": counted("a_emptied_vec")})
        A0 = Banks(front_fills, 2, counted("first_filled"),
                   {"act": counted("first_emptied_act"), "vec": counted("first_emptied_vec")})
        def max_fills(heads):
            return [(("max", h, it), "vec") for h in heads for it in range(IT)]

        def score_fills(steps):
            return [(("score", n, g), "act") for n in steps for g in range(4)]

        MAX_AND_SCORES = max_fills(range(4)) + [(("max_t", 0), "act")] + max_fills((4, 5)) + score_fills((0,)) \
            + max_fills((6,)) + score_fills((1,)) + max_fills((7,)) + [(("max_t", 1), "act")] \
            + score_fills(range(2, NS))
        Bb = Banks(
            [(("feat", m), "act") for m in range(KT)] + [(("q", m), "act") for m in range(KT)]
            + [(("ac",), "act")] + [(("k", m), "act") for m in range(KT)] + [(("v", n), "vec") for n in range(2)]
            + MAX_AND_SCORES
            + [(("den",), "vec")] + [(("back", n), "vec") for n in range(2)],
            2, counted("b_filled"), {"act": counted("b_emptied_act"), "vec": counted("b_emptied_vec")})

        def bank_a(ring, key):
            return ring_a[:, ring.bank(key), :]

        def bank_b(key):
            return ring_b[:, Bb.bank(key), :]

        def as_rows(bank):
            return bank.rearrange("p (t d) -> p t d", d=D)

        def as_heads(rows):
            return rows.rearrange("p t (h d) -> p t h d", d=DH)

        def by_feature(w):
            return w.rearrange("(k p) n -> p k n", p=P)

        def column(v):
            return v.rearrange("(k p) -> p k", p=P)

        weight_loads = [(w1[:], by_feature(W1)), (w2[:], by_feature(W2)), (wq[:], by_feature(W_q)),
                        (wk[:], by_feature(W_k)), (wv[:], by_feature(W_v))]
        weight_loads += [(gb[:, n, :], column(v)) for n, v in enumerate((g1, b1, g2, b2))]
        weight_loads += [(qk_bias[:, n, :], column(v)) for n, v in enumerate((b_q, b_k))]
        weight_loads += [(a_rows[:, n, :], v.rearrange("h d -> (h d)").partition_broadcast(P))
                         for n, v in enumerate((a_src1, a_dst1, a_src2, a_dst2))]
        weight_loads += [(bv[:], b_v.partition_broadcast(P))]
        gate = w_g.rearrange("(s k p) -> p s k", p=P, k=KT)
        late_loads = [(bg[0:1, :], b_g.rearrange("(a b) -> a b", a=1))]
        late_loads += [(wg[:, k, 32 * s:32 * s + 1], gate[:, s, k:k + 1]) for s in range(2) for k in range(KT)]
        N_WEIGHT_LOADS = len(weight_loads) + len(late_loads)
        CONSTS = 18

        x_tiles = x.rearrange("b (t p) d -> b p t d", p=P)
        adj_tiles = adj.rearrange("b (t p) n -> b p t n", p=P)
        out_tiles = out.rearrange("b (t p) d -> b p t d", p=P)

        def loop(eng, first, pair, last):
            first(Batch(0), Batch(0, 1))
            with eng.Fori(0, B - 1) as i:
                pair(Batch(i, 2), Batch(i, 1), Batch(i))
            last(Batch(B - 1))

        block = ctx.enter_context(nc.Block())

        @block.sync
        def _(sp):
            for s in loop_sems:
                sp.sem_inc(s, START)
            for dst, src in weight_loads:
                sp.dma_start(dst, src, allow_slow_non_contiguous=True).then_inc(weights_loaded, 16)
            sp.dma_start(adj_rows[:], adj_tiles[0]).then_inc(adj_loaded, 16)
            sp.dma_start(x_rows[:], x_tiles[0]).then_inc(x_loaded, 16)
            sp.wait_ge(consts_made, CONSTS)
            for dst, src in late_loads:
                sp.dma_start(dst, src, allow_slow_non_contiguous=True).then_inc(weights_loaded, 16)
            q_raw, k_raw = q_stack[:].bitcast(F32), k_stack[:].bitcast(F32)
            sp.dma_start(k_raw[96:98, :, :], ones_row.unsqueeze(1).broadcast_to((2, H, N))).then_inc(stack_consts, 16)
            sp.dma_start(q_raw[98:100, :, :], ones_row.unsqueeze(1).broadcast_to((2, H, N))).then_inc(stack_consts, 16)
            for n in range(N // P):
                sp.dma_start(k_raw[104:104 + H, :, n * P:(n + 1) * P], minus_head_f32).then_inc(stack_consts, 16)

            def load_x(b, n):
                sp.wait_ge(x2_ready, b.count(IT // 2, IT // 2))
                sp.dma_start(x_rows[:], x_tiles[n]).then_inc(x_loaded, 16)

            def load_adj(n):
                sp.dma_start(adj_rows[:], adj_tiles[n]).then_inc(adj_loaded, 16)

            def load_adj_again(b, after, n):
                sp.wait_ge(exp_adj_ready, after.count(IT, IT))
                sp.dma_start(adj_rows[:], adj_tiles[n]).then_inc(adj_loaded_again, 16)

            def move(rows, n, part, g):
                sp.dma_start(rows[32 * n:32 * n + 32, g:H:4, :],
                             part[32 * g:32 * g + 32, :, :].bitcast(F32)).then_inc(strip_loaded[g], 16)

            def queries_and_gates(b):
                Bb.wait_emptied(sp, b, ("q", KT - 1))
                for n in range(2):
                    for g in range(4):
                        move(q_raw, n, q_hi, g)
                sp.wait_ge(parts_split, b.count(3, 1))
                for g in range(4):
                    move(q_raw, 2, q_lo, g)
                sp.wait_ge(parts_split, b.count(3, 2))
                for n, (rows, part, r) in enumerate(((q_raw, ac_hi, 0), (q_raw, ac_lo, 0),
                                                     (k_raw, ac_hi, 32), (k_raw, ac_lo, 32))):
                    sp.dma_start(rows[96 + n:97 + n, :, :],
                                 part[r:r + 1, :].bitcast(F32).unsqueeze(1).broadcast_to((1, H, N))
                                 ).then_inc(gates_loaded, 16)

            def keys(b):
                sp.wait_ge(parts_split, b.count(3, 3))
                for g in range(4):
                    for n, part in enumerate((k_hi, k_lo, k_hi)):
                        move(k_raw, n, part, g)

            def maxima(b, q):
                Bb.wait_emptied(sp, b, ("max_t", q))
                sp.dma_start(q_raw[104 + 4 * q:108 + 4 * q, 4 * q:4 * q + 4, :],
                             max_t[:, q, :].bitcast(F32).unsqueeze(1).broadcast_to((4, 4, N))
                             ).then_inc(max_loaded, 16)

            def store(b, n):
                sp.wait_ge(out_ready, b.count(IT // 2, IT // 2))
                sp.dma_start(out_tiles[n], out_rows).then_inc(stored, 16)

            sp.wait_ge(exp_adj_ready, Batch(0).count(IT, IT))
            load_adj(1)
            load_x(Batch(0), 1)
            load_adj_again(Batch(0), Batch(1), 0)

            def round_of(n, a, b, into, again, source):
                A.wait_filled(sp, b, ("adj_t", IT - 1))
                load_adj(source)
                load_x(a, source)
                queries_and_gates(b)
                keys(b)
                load_adj_again(a, n, again)
                maxima(b, 0)
                maxima(b, 1)
                store(b, into)

            with sp.Fori(0, B - 2) as i:
                round_of(Batch(i, 2), Batch(i, 1), Batch(i), i, i + 1, i + 2)
            round_of(Batch(B), Batch(B - 1), Batch(B - 2), B - 2, B - 1, B - 1)
            queries_and_gates(Batch(B - 1))
            keys(Batch(B - 1))
            maxima(Batch(B - 1), 0)
            maxima(Batch(B - 1), 1)
            store(Batch(B - 1), B - 1)
            sp.wait_ge(stored, 16 * B + START)

        @block.gpsimd
        def _(pool):
            for tile, value in ((ident[:], 0.0), (select_f32, 0.0), (minus_head_f32, 0.0), (ones_row, 1.0),
                                (ones[:], 0.0), (minus_half[:], -0.5), (wg[:], 0.0), (bg[:], 0.0),
                                (fc_rows[:], 0.0), (c1[:], 0.0)):
                pool.memset(tile, value).then_inc(consts_made, 1)
            pool.wait_ge(consts_made, 10)
            pool.affine_select(out=ident[:], in_=ident[:], compare_op=ALU.not_equal, fill=1.0, base=0,
                               pattern=[[-1, P]], channel_multiplier=1).then_inc(consts_made, 1)
            pool.affine_select(out=select_f32, in_=select_f32, compare_op=ALU.not_equal, fill=1.0, base=-64,
                               pattern=[[-1, H], [0, P]], channel_multiplier=1).then_inc(consts_made, 1)
            pool.affine_select(out=minus_head_f32, in_=minus_head_f32, compare_op=ALU.not_equal, fill=-1.0,
                               base=0, pattern=[[-1, H], [0, P]], channel_multiplier=1).then_inc(consts_made, 1)
            for q in range(QUADS):
                pool.memset(ones[:, q, q * HALF:(q + 1) * HALF], 1.0).then_inc(consts_made, 1)
            pool.wait_ge(consts_made, 15)
            pool.affine_select(out=select_f32, in_=select_f32, compare_op=ALU.not_equal, fill=1.0, base=-96,
                               pattern=[[-1, H], [0, P]], channel_multiplier=1).then_inc(consts_made, 1)
            for n, rows in enumerate((q_stack, k_stack)):
                pool.wait_ge(consts_made, 16 + n)
                pool.memset(rows[96:P, :, :].bitcast(F32), 0.0).then_inc(consts_made, 1)
            pool.wait_ge(consts_made, CONSTS)

            def inverse_deviation(b, layer):
                pool.wait_ge(var_ready, b.count(2, layer + 1))
                pool.tensor_tensor(rstd[:, layer, :], var_eps[:, layer, :], minus_half[:],
                                   ALU.pow).then_inc(rstd_ready, 1)

            def low_part(b, name, high, low):
                for m in range(KT):
                    Bb.wait_emptied(pool, b, (name, m))
                    ins = pool.tensor_tensor(low[:, m, :], qk_f32[:, m, :], high[:, m, :].bitcast(F32),
                                             ALU.subtract)
                ins.then_inc(parts_split, 1)

            def low_gates(b):
                pool.wait_ge(parts_split, b.count(3, 1))
                Bb.wait_emptied(pool, b, ("ac",))
                pool.tensor_tensor(ac_lo, ac_f32[:], ac_hi.bitcast(F32), ALU.subtract).then_inc(parts_split, 1)
                pool.wait_ge(parts_split, b.count(3, 2))

            def multiply(b, n):
                Bb.wait_emptied(pool, b, ("score", n, 3))
                p = probs_b[:, n % B_BUFS, :, :]
                jt = STEPS[n][1]
                pool.tensor_tensor(p, p, adj_t[:, jt:jt + 1, :].broadcast_to((P, 4, N)),
                                   ALU.mult).then_inc(probs_b_pool, 1)

            def first(a, n):
                inverse_deviation(a, 0)
                inverse_deviation(a, 1)
                inverse_deviation(n, 0)

            def pair(n, a, b):
                inverse_deviation(a, 1)
                low_part(b, "q", q_hi, q_lo)
                low_gates(b)
                low_part(b, "k", k_hi, k_lo)
                inverse_deviation(n, 0)
                for s in POOL_STEPS:
                    multiply(b, s)

            def last(b):
                low_part(b, "q", q_hi, q_lo)
                low_gates(b)
                low_part(b, "k", k_hi, k_lo)
                for n in POOL_STEPS:
                    multiply(b, n)

            loop(pool, first, pair, last)

        @block.scalar
        def _(act):
            act.wait_ge(weights_loaded, 16 * N_WEIGHT_LOADS)
            act.mul(qk_bias[:, 2, :], qk_bias[:, 0, :], SCALE).then_inc(scaled_bias, 1)
            act.wait_ge(scaled_bias, 1)
            b_done = Bb.emptied["act"]

            def a_features(ring, r, layer):
                for m in range(KT):
                    key = ("feat", layer, m)
                    ring.wait_filled(act, r, key)
                    nc.scalar.activation((feat_b, feat_a)[layer][:, m, :], bank_a(ring, key), ACT.Identity,
                                         bias=gb[:, 2 * layer + 1, m:m + 1],
                                         scale=gb[:, 2 * layer, m:m + 1]).then_inc(ring.emptied["act"], 1)

            def exp_adjacency(b, before):
                act.wait_ge(adj_max_ready, b.count(IT, IT))
                if before is not None:
                    act.wait_ge(probs_a_used, before.count(A_PROBS, NS))
                for it in range(IT):
                    nc.scalar.activation(exp_adj[:, it, :], adj_rows[:, it, :], ACT.Exp,
                                         bias=neg_adj_max[:, it:it + 1]).then_inc(exp_adj_ready, 1)

            def exp_adjacency_turned(ring, r, b):
                act.wait_ge(probs_a_ready, b.count(A_PROBS))
                for jt in range(IT):
                    ring.wait_filled(act, r, ("exp_t", jt))
                    nc.scalar.activation(exp_adj_t[:, jt, :], bank_a(ring, ("exp_t", jt)),
                                         ACT.Copy).then_inc(ring.emptied["act"], 1)

            def factor_rows(ring, r, b, layer):
                heads = H if layer == 0 else 1
                act.wait_ge(t_max_ready, b.count(2, layer + 1))
                bank = bank_a(ring, ("st", layer))
                nc.scalar.activation(fc_rows[64:64 + heads, :], bank[0:heads, :], ACT.Exp,
                                     bias=t_max[0:heads, 2:3], scale=1.0 - SLOPE)
                nc.scalar.activation(g_hl[64:64 + heads, :], bank[0:heads, :], ACT.Exp,
                                     bias=t_max[0:heads, 2:3], scale=1.0 - SLOPE).then_inc(exp_rows_ready, 1)
                nc.scalar.activation(fc_rows[0:heads, :], bank[32:32 + heads, :], ACT.Exp,
                                     bias=t_max[32:32 + heads, 1:2])
                nc.scalar.activation(fc_rows[32:32 + heads, :], bank[32:32 + heads, :], ACT.Exp,
                                     bias=t_max[32:32 + heads, 2:3], scale=-(1.0 - SLOPE)).then_inc(ring.emptied["act"], 1)

            def factor_columns(ring, r, layer):
                ring.wait_filled(act, r, ("cols", layer))
                nc.scalar.activation(fc_cols[:, layer, :, :],
                                     bank_a(ring, ("cols", layer)).rearrange("p (t c) -> p t c", c=P)[:, :, 0:64],
                                     ACT.Copy).then_inc(ring.emptied["act"], 1)

            def g_everywhere(ring, r, h):
                ring.wait_filled(act, r, ("g", h))
                nc.scalar.activation(g_all[:, h, :], bank_a(ring, ("g", h)), ACT.Copy).then_inc(ring.emptied["act"], 1)

            def g_everywhere_2(b):
                A.wait_filled(act, b, ("g2",))
                nc.scalar.activation(g_2[:], bank_a(A, ("g2",)), ACT.Copy).then_inc(A.emptied["act"], 1)

            def values_2(b):
                for n in range(2):
                    A.wait_filled(act, b, ("h", 1, n))
                    for t in range(2):
                        it = 2 * n + t
                        ins = nc.scalar.activation(v2[:, it, 0:D], as_rows(bank_a(A, ("h", 1, n)))[:, t, :],
                                                   ACT.Identity, scale=fc_cols[:, 1, it, 0:1])
                    ins.then_inc(A.emptied["act"], 1)

            def a_heads(b, q):
                act.wait_ge(probs_a_used, b.count(A_PROBS, (q + 1) * IT))
                last = q == QUADS - 1
                nc.scalar.activation(num_a[:, q, :], heads_a[:, 0, :], ACT.Copy).then_inc(heads_a_emptied, 1)
                if last:
                    nc.scalar.activation(den_a[:], heads_a[:, 1, :], ACT.Copy).then_inc(heads_a_emptied, 1)

            def keep_x3(b):
                act.wait_ge(out_ready, b.count(IT // 2))
                act.wait_ge(rows2_emptied, b.count(IT, IT))
                nc.scalar.activation(x3[:], x2[:], ACT.Copy).then_inc(x3_ready, 1)

            def adjacency_turned(b, multiplied):
                if multiplied is not None:
                    act.wait_ge(probs_b_vec, multiplied.count(len(DVE_STEPS), len(DVE_STEPS)))
                    act.wait_ge(probs_b_pool, multiplied.count(len(POOL_STEPS), len(POOL_STEPS)))
                for jt in range(IT):
                    A.wait_filled(act, b, ("adj_t", jt))
                    nc.scalar.activation(adj_t[:, jt, :], bank_a(A, ("adj_t", jt)), ACT.Copy,
                                         bias=ADJ_EPS).then_inc(A.emptied["act"], 1)

            def b_features(b):
                for m in range(KT):
                    Bb.wait_filled(act, b, ("feat", m))
                    nc.scalar.activation(feat_b[:, m, :], bank_b(("feat", m)), ACT.Copy).then_inc(b_done, 1)

            def q_or_k(b, name):
                high, bias, scale = (q_hi, 2, SCALE) if name == "q" else (k_hi, 1, 1.0)
                if name == "q":
                    for loaded in strip_loaded:
                        act.wait_ge(loaded, b.count(16 * 6))
                    act.wait_ge(stored, b.count(16))
                else:
                    act.wait_ge(parts_split, b.count(3, 1))
                for m in range(KT):
                    Bb.wait_filled(act, b, (name, m))
                    nc.scalar.activation(qk_f32[:, m, :], bank_b((name, m)), ACT.Identity,
                                         bias=qk_bias[:, bias, m:m + 1], scale=scale)
                    nc.scalar.activation(high[:, m, :], bank_b((name, m)), ACT.Identity,
                                         bias=qk_bias[:, bias, m:m + 1], scale=scale).then_inc(b_done, 1)

            def gate_rows(b):
                act.wait_ge(gates_loaded, b.count(16 * 4))
                Bb.wait_filled(act, b, ("ac",))
                nc.scalar.activation(ac_f32[:], bank_b(("ac",))[0:64, :], ACT.Identity, bias=bg[:])
                nc.scalar.activation(ac_hi, bank_b(("ac",))[0:64, :], ACT.Identity, bias=bg[:]).then_inc(b_done, 1)

            def maxima(b, q):
                act.wait_ge(max_loaded, b.count(16 * QUADS))
                Bb.wait_filled(act, b, ("max_t", q))
                nc.scalar.activation(max_t[:, q, :], bank_b(("max_t", q))[0:4, :], ACT.Copy).then_inc(b_done, 1)

            def exp_scores(b, n):
                if n >= B_BUFS:
                    act.wait_ge(probs_b_used, b.count(NS, n - B_BUFS + 1))
                else:
                    act.wait_ge(probs_b_used, b.count(NS))
                for g in range(4):
                    Bb.wait_filled(act, b, ("score", n, g))
                    nc.scalar.activation(probs_b[:, n % B_BUFS, g, :], bank_b(("score", n, g)),
                                         ACT.Exp).then_inc(b_done, 1)

            def b_heads(b, q):
                act.wait_ge(probs_b_used, b.count(NS, (q + 1) * IT))
                nc.scalar.activation(num_b[:, q, :], heads_b[:, 0, :], ACT.Copy).then_inc(heads_b_emptied, 1)
                if q == QUADS - 1:
                    nc.scalar.activation(den_b, heads_b[:, 1, :], ACT.Copy).then_inc(heads_b_emptied, 1)

            def b_front(b):
                b_features(b)
                q_or_k(b, "q")
                gate_rows(b)
                keep_x3(b)
                q_or_k(b, "k")

            def first(a, n):
                exp_adjacency(a, None)
                a_features(A0, a, 0)
                factor_rows(A0, a, a, 0)
                exp_adjacency_turned(A0, a, a)
                factor_columns(A0, a, 0)
                for h in range(H):
                    g_everywhere(A0, a, h)
                a_heads(a, 0)
                a_heads(a, 1)
                a_features(A, a, 1)
                exp_adjacency(n, a)
                factor_rows(A, a, a, 1)
                factor_columns(A, a, 1)
                g_everywhere_2(a)
                values_2(a)
                a_features(A, a, 0)
                factor_rows(A, a, n, 0)
                exp_adjacency_turned(A, a, n)
                factor_columns(A, a, 0)
                for h in range(H):
                    g_everywhere(A, a, h)
                a_heads(n, 0)
                a_heads(n, 1)
                adjacency_turned(a, None)

            def pair(n, a, b):
                keep_x3(b)
                b_features(b)
                q_or_k(b, "q")
                gate_rows(b)
                q_or_k(b, "k")
                a_features(A, a, 1)
                factor_rows(A, a, a, 1)
                factor_columns(A, a, 1)
                g_everywhere_2(a)
                values_2(a)
                a_features(A, a, 0)
                exp_adjacency(n, a)
                factor_rows(A, a, n, 0)
                exp_adjacency_turned(A, a, n)
                factor_columns(A, a, 0)
                g_everywhere(A, a, 0)
                g_everywhere(A, a, 1)
                maxima(b, 0)
                g_everywhere(A, a, 2)
                g_everywhere(A, a, 3)
                for h in range(4, H):
                    g_everywhere(A, a, h)
                exp_scores(b, 0)
                exp_scores(b, 1)
                maxima(b, 1)
                exp_scores(b, 2)
                exp_scores(b, 3)
                exp_scores(b, 4)
                a_heads(n, 0)
                exp_scores(b, 5)
                b_heads(b, 0)
                exp_scores(b, 6)
                exp_scores(b, 7)
                adjacency_turned(a, b)
                b_heads(b, 1)
                a_heads(n, 1)

            def last(b):
                b_front(b)
                maxima(b, 0)
                exp_scores(b, 0)
                exp_scores(b, 1)
                maxima(b, 1)
                for n in range(2, 6):
                    exp_scores(b, n)
                b_heads(b, 0)
                exp_scores(b, 6)
                exp_scores(b, 7)
                b_heads(b, 1)

            loop(act, first, pair, last)

        @block.vector
        def _(dve):
            dve.wait_ge(consts_made, CONSTS)
            nc.vector.tensor_copy(select_head[:], select_f32).then_inc(rounded_consts, 1)
            nc.vector.memset(g_hl[:].bitcast(F32), 0.0)
            nc.vector.memset(wa1[:], 0.0)
            nc.vector.memset(wa2[:], 0.0).then_inc(vec_cleared, 1)
            dve.wait_ge(weights_loaded, 16 * N_WEIGHT_LOADS)
            dve.wait_ge(vec_cleared, 1)
            n = 0
            for layer, (w, wa, heads) in enumerate(((w1, wa1, H), (w2, wa2, 1))):
                for side in range(2):
                    for k in range(KT):
                        if n > 0:
                            dve.wait_ge(wa_ready, n)
                        nc.vector.tensor_tensor(wa_tmp, w[:, k, :], a_rows[:, 2 * layer + side, :],
                                                ALU.mult).then_inc(wa_products, 1)
                        dve.wait_ge(wa_products, n + 1)
                        nc.vector.tensor_reduce(wa[:, k, 32 * side:32 * side + heads],
                                                wa_tmp.rearrange("p (h d) -> p h d", h=heads),
                                                AX_X, ALU.add).then_inc(wa_ready, 1)
                        n += 1
            a_done, b_done = A.emptied["vec"], Bb.emptied["vec"]

            def layer_norm(b, layer):
                rows = x_rows if layer == 0 else x2
                if layer == 0:
                    dve.wait_ge(x_loaded, b.count(16, 16))
                for it in range(IT):
                    ins = nc.vector.bn_stats(stats[:, it, :], rows[:, it, :])
                ins.then_inc(stats_ready, 1)
                dve.wait_ge(stats_ready, b.count(2, layer + 1))
                nc.vector.memset(spare[:], 0.0)
                for it in range(IT):
                    ins = nc.vector.bn_aggr(mean_var[:, it, :], stats[:, it, :])
                ins.then_inc(mean_ready, 1)
                dve.wait_ge(mean_ready, b.count(2, layer + 1))
                nc.vector.tensor_scalar(var_eps[:, layer, :], mean_var[:, :, 1], LN_EPS, None,
                                        ALU.add).then_inc(var_ready, 1)

            def normalise(b, layer):
                rows, normal = ((x_rows, normed_1), (x2, normed))[layer]
                dve.wait_ge(rstd_ready, b.count(2, layer + 1))
                for it in range(IT):
                    nc.vector.tensor_scalar(normal[:, it, :], rows[:, it, :], mean_var[:, it, 0:1],
                                            rstd[:, layer, it:it + 1], ALU.subtract,
                                            ALU.mult).then_inc(normed_ready, 1)

            def adjacency_maxima(b, it):
                if it == 0:
                    dve.wait_ge(adj_loaded, b.count(16, 16))
                    dve.wait_ge(exp_adj_ready, b.count(IT))
                nc.vector.tensor_reduce(neg_adj_max[:, it:it + 1], adj_rows[:, it, :], AX_X, ALU.max,
                                        negate=True).then_inc(adj_max_ready, 1)

            def target_maximum(ring, r, b, layer):
                heads = H if layer == 0 else 1
                ring.wait_filled(dve, r, ("st", layer))
                nc.vector.tensor_reduce(t_max[32:32 + heads, 0:1], bank_a(ring, ("st", layer))[32:32 + heads, :],
                                        AX_X, ALU.max).then_inc(target_max_found, 1)
                dve.wait_ge(target_max_found, b.count(2, layer + 1))
                nc.vector.tensor_scalar(t_max[32:32 + heads, 1:2], t_max[32:32 + heads, 0:1], -1.0, None, ALU.mult)
                nc.vector.tensor_scalar(t_max[32:32 + heads, 2:3], t_max[32:32 + heads, 0:1], 1.0 - SLOPE, None,
                                        ALU.mult)
                nc.vector.tensor_scalar(t_max[0:heads, 2:3], t_max[32:32 + heads, 0:1], 1.0 - SLOPE, None,
                                        ALU.mult).then_inc(t_max_ready, 1)

            def g_low_part(b, layer):
                heads = H if layer == 0 else 1
                dve.wait_ge(exp_rows_ready, b.count(2, layer + 1))
                nc.vector.tensor_tensor(g_hl[96:96 + heads, :], fc_rows[64:64 + heads, :],
                                        g_hl[64:64 + heads, :].bitcast(F32), ALU.subtract).then_inc(g_split, 1)

            def values_1(ring, r):
                ring.wait_emptied(dve, r, ("cols", 0))
                c = fc_cols[:, 0, :, 0:H].unsqueeze(3)
                for q in range(QUADS):
                    hs = slice(4 * q, 4 * q + 4)
                    nc.vector.tensor_copy(c1[:, :, hs, q * HALF:(q + 1) * HALF],
                                          c[:, :, hs, :].broadcast_to((P, IT, 4, HALF)))
                for n in range(2):
                    ring.wait_filled(dve, r, ("h", 0, n))
                    nc.vector.tensor_tensor(v1[:, 2 * n:2 * n + 2, :, :], as_heads(as_rows(bank_a(ring, ("h", 0, n)))),
                                            c[:, 2 * n:2 * n + 2, :, :].broadcast_to((P, 2, H, DH)),
                                            ALU.mult).then_inc(ring.emptied["vec"], 1)

            def weights_1(ring, r, b, n):
                q, jt = STEPS[n]
                if jt == 0:
                    ring.wait_emptied(dve, r, ("g", 4 * q + 3))
                if n >= A_BUFS:
                    dve.wait_ge(probs_a_used, b.count(A_PROBS, n - A_BUFS + 1))
                elif n == 0:
                    dve.wait_ge(probs_a_used, b.count(A_PROBS))
                for g in range(4):
                    h = 4 * q + g
                    ins = nc.vector.scalar_tensor_tensor(
                        probs_a[:, n % A_BUFS, g, :], g_all[:, h, :], fc_cols[:, 0, jt, 32 + h:33 + h],
                        exp_adj_t[:, jt, :], ALU.max, ALU.mult)
                ins.then_inc(probs_a_ready, 1)

            def heads_reciprocal(ring, b, bank, recip, done):
                ring.wait_filled(dve, b, ("den",))
                nc.vector.reciprocal(recip[:].rearrange("p t q g -> p t g q"),
                                     bank.rearrange("p (t g q r) -> p t g q r", t=IT, g=4, q=QUADS)[:, :, :, :, 0]
                                     ).then_inc(done, 1)
                ring.wait_emptied(dve, b, ("den",))

            def normalised_rows(ring, b, n, bank, recip, into, done):
                ring.wait_filled(dve, b, ("back", n))
                nc.vector.tensor_tensor(as_heads(into[:, 2 * n:2 * n + 2, :]), as_heads(as_rows(bank)),
                                        recip[:, 2 * n:2 * n + 2, :, :].rearrange("p t q g -> p t (q g)").unsqueeze(3)
                                        .broadcast_to((P, 2, H, DH)), ALU.mult).then_inc(done, 1)

            def first_layer_rows(b, before):
                heads_reciprocal(A, b, bank_a(A, ("den",)), recip_a, a_done)
                dve.wait_ge(x3_ready, b.count(1))
                if before is not None:
                    Bb.wait_filled(dve, before, ("feat", KT - 1))
                for n in range(2):
                    rows = slice(2 * n, 2 * n + 2)
                    normalised_rows(A, b, n, bank_a(A, ("back", n)), recip_a, x2, a_done)
                    A.wait_emptied(dve, b, ("back", n))
                    nc.vector.tensor_tensor(x2[:, rows, :], x2[:, rows, :], x_rows[:, rows, :],
                                            ALU.add).then_inc(x2_ready, 1)
                dve.wait_ge(x2_ready, b.count(IT // 2, IT // 2))

            def weights_of_c_2(b):
                A.wait_emptied(dve, b, ("cols", 1))
                nc.vector.tensor_copy(v2[:, :, D:D + 2], fc_cols[:, 1, :, 0:1].broadcast_to((P, IT, 2)))

            def weights_2(b):
                A.wait_emptied(dve, b, ("g2",))
                dve.wait_ge(probs_a_used, b.count(A_PROBS, NS))
                for jt in range(IT):
                    ins = nc.vector.scalar_tensor_tensor(
                        probs_a[:, NS % A_BUFS, jt, :], g_2[:], fc_cols[:, 1, jt, 32:33],
                        exp_adj_t[:, jt, :], ALU.max, ALU.mult)
                ins.then_inc(probs_a_ready, 1)

            def second_layer_rows(b, it):
                if it < IT - 1:
                    dve.wait_ge(rows2_filled, b.count(IT - 1, it + 1))
                else:
                    dve.wait_ge(probs_a_used, b.count(A_PROBS, A_PROBS))
                nc.vector.reciprocal(recip_2[:, it:it + 1], heads_a[:, it % 2, D:D + 1]).then_inc(recip_2_ready, 1)
                dve.wait_ge(recip_2_ready, b.count(IT, it + 1))
                nc.vector.scalar_tensor_tensor(x2[:, it, :], heads_a[:, it % 2, 0:D], recip_2[:, it:it + 1],
                                               x2[:, it, :], ALU.mult, ALU.add).then_inc(rows2_emptied, 1)

            def values_3(b):
                for n in range(2):
                    Bb.wait_filled(dve, b, ("v", n))
                    nc.vector.tensor_tensor(v3[:, 2 * n:2 * n + 2, :], as_rows(bank_b(("v", n))),
                                            bv[:].unsqueeze(1).broadcast_to((P, 2, D)), ALU.add).then_inc(b_done, 1)

            def maxima(b, h, tiles=range(IT)):
                for it in tiles:
                    Bb.wait_filled(dve, b, ("max", h, it))
                    nc.vector.tensor_reduce(row_max[:, it, h:h + 1], bank_b(("max", h, it)),
                                            AX_X, ALU.max).then_inc(b_done, 1)

            def multiply(b, n):
                Bb.wait_emptied(dve, b, ("score", n, 3))
                p = probs_b[:, n % B_BUFS, :, :]
                jt = STEPS[n][1]
                nc.vector.tensor_tensor(p, p, adj_t[:, jt:jt + 1, :].broadcast_to((P, 4, N)),
                                        ALU.mult).then_inc(probs_b_vec, 1)

            def attention_rows(b):
                heads_reciprocal(Bb, b, bank_b(("den",)), recip_b, b_done)
                for n in range(2):
                    rows = slice(2 * n, 2 * n + 2)
                    normalised_rows(Bb, b, n, bank_b(("back", n)), recip_b, out_rows, b_done)
                    Bb.wait_emptied(dve, b, ("back", n))
                    nc.vector.tensor_tensor(out_rows[:, rows, :], out_rows[:, rows, :], x3[:, rows, :],
                                            ALU.add).then_inc(out_ready, 1)

            def first(a, n):
                for it in range(IT):
                    adjacency_maxima(a, it)
                layer_norm(a, 0)
                normalise(a, 0)
                target_maximum(A0, a, a, 0)
                g_low_part(a, 0)
                values_1(A0, a)
                for s in range(NS):
                    weights_1(A0, a, a, s)
                first_layer_rows(a, None)
                layer_norm(a, 1)
                for it in range(IT):
                    adjacency_maxima(n, it)
                normalise(a, 1)
                target_maximum(A, a, a, 1)
                g_low_part(a, 1)
                weights_of_c_2(a)
                weights_2(a)
                layer_norm(n, 0)
                normalise(n, 0)
                target_maximum(A, a, n, 0)
                g_low_part(n, 0)
                for it in range(IT):
                    second_layer_rows(a, it)
                values_1(A, a)
                for s in range(NS):
                    weights_1(A, a, n, s)

            def pair(n, a, b):
                def weights(s):
                    weights_1(A, a, n, s)

                first_layer_rows(a, b)
                layer_norm(a, 1)
                for it in range(IT):
                    adjacency_maxima(n, it)
                normalise(a, 1)
                layer_norm(n, 0)
                target_maximum(A, a, a, 1)
                normalise(n, 0)
                g_low_part(a, 1)
                values_3(b)
                weights_of_c_2(a)
                weights_2(a)
                maxima(b, 0)
                second_layer_rows(a, 0)
                maxima(b, 1, (0, 1))
                target_maximum(A, a, n, 0)
                maxima(b, 1, (2, 3))
                second_layer_rows(a, 1)
                g_low_part(n, 0)
                maxima(b, 2)
                second_layer_rows(a, 2)
                maxima(b, 3, (0, 1))
                second_layer_rows(a, 3)
                maxima(b, 3, (2, 3))
                maxima(b, 4)
                values_1(A, a)
                maxima(b, 5)
                weights(0)
                maxima(b, 6)
                weights(1)
                maxima(b, 7)
                weights(2)
                weights(3)
                weights(4)
                multiply(b, 4)
                weights(5)
                multiply(b, 5)
                weights(6)
                multiply(b, 7)
                weights(7)
                attention_rows(b)

            def last(b):
                values_3(b)
                for h in range(H):
                    maxima(b, h)
                for n in DVE_STEPS:
                    multiply(b, n)
                attention_rows(b)

            loop(dve, first, pair, last)

        @block.tensor
        def _(pe):
            pe.wait_ge(consts_made, CONSTS)
            pe.wait_ge(rounded_consts, 1)
            pe.wait_ge(wa_ready, 8)
            pe.wait_ge(stack_consts, 16 * (2 + N // P))

            def turn(bank, rows, m, it):
                return nc.tensor.transpose(bank[:, it * P:(it + 1) * P], rows[:, it, m * P:(m + 1) * P], ident[:])

            def a_features(ring, r, b, layer):
                for m in range(KT):
                    ring.wait_free(pe, r, ("feat", layer, m))
                    for it in range(IT):
                        if m == 0:
                            pe.wait_ge(normed_ready, b.count(2 * IT, layer * IT + it + 1))
                        mm = turn(bank_a(ring, ("feat", layer, m)), (normed_1, normed)[layer], m, it)
                    mm.then_inc(ring.filled, 1)

            def source_and_target(ring, r, layer):
                ring.wait_free(pe, r, ("st", layer))
                wa = wa1 if layer == 0 else wa2
                for k in range(KT):
                    ring.wait_emptied(pe, r, ("feat", layer, k))
                    mm = nc.tensor.matmul(bank_a(ring, ("st", layer))[0:64, :], wa[:, k, :],
                                          (feat_b, feat_a)[layer][:, k, :],
                                          start=(k == 0), stop=(k == KT - 1))
                mm.then_inc(ring.filled, 1)

            def turn_exp_adjacency(ring, r, b):
                for jt in range(IT):
                    ring.wait_free(pe, r, ("exp_t", jt))
                    for it in range(IT):
                        if jt == 0:
                            pe.wait_ge(exp_adj_ready, b.count(IT, it + 1))
                        mm = turn(bank_a(ring, ("exp_t", jt)), exp_adj, jt, it)
                    mm.then_inc(ring.filled, 1)

            def factor_columns(ring, r, layer):
                ring.wait_free(pe, r, ("cols", layer))
                ring.wait_emptied(pe, r, ("st", layer))
                for jt in range(IT):
                    mm = nc.tensor.transpose(bank_a(ring, ("cols", layer))[:, P * jt:P * jt + P],
                                             fc_rows[:, jt * P:(jt + 1) * P], ident[:])
                mm.then_inc(ring.filled, 1)

            def rows_times(ring, r, key, bank, features, w, n):
                ring.wait_free(pe, r, key)
                for t in range(2):
                    for k in range(KT):
                        it = 2 * n + t
                        mm = nc.tensor.matmul(as_rows(bank)[:, t, :], features[:, k, it * P:(it + 1) * P],
                                              w[:, k, :], start=(k == 0), stop=(k == KT - 1))
                mm.then_inc(ring.filled, 1)

            def values_1(ring, r, halves=(0, 1)):
                for n in halves:
                    rows_times(ring, r, ("h", 0, n), bank_a(ring, ("h", 0, n)), feat_b, w1, n)

            def values_2(b, halves=(0, 1)):
                for n in halves:
                    rows_times(A, b, ("h", 1, n), bank_a(A, ("h", 1, n)), feat_a, w2, n)

            def g_everywhere(ring, r, b, h):
                ring.wait_free(pe, r, ("g", h))
                if h == 0:
                    pe.wait_ge(g_split, b.count(2, 1))
                nc.tensor.matmul(bank_a(ring, ("g", h)), select_head[:, h, :], g_hl[:], start=True,
                                 stop=True).then_inc(ring.filled, 1)

            def g_everywhere_2(b):
                A.wait_free(pe, b, ("g2",))
                pe.wait_ge(g_split, b.count(2, 2))
                nc.tensor.matmul(bank_a(A, ("g2",)), select_head[:, 0, :], g_hl[:], start=True,
                                 stop=True).then_inc(A.filled, 1)

            def four_heads(banks, probs, n, which, stationary):
                q, jt = STEPS[n]
                for g in range(4):
                    mm = nc.tensor.matmul(
                        banks[32 * g:32 * g + 32, which, :], stationary(q, jt, 4 * q + g), probs[:, g, :],
                        start=(n == 0 if which else jt == 0), stop=(n == NS - 1 if which else jt == IT - 1),
                        tile_position=(0, 32 * g))
                return mm

            def a_numerators(ring, r, b, n):
                pe.wait_ge(probs_a_ready, b.count(A_PROBS, n + 1))
                if n == 0:
                    pe.wait_ge(rows2_emptied, b.count(IT))
                    ring.wait_emptied(pe, r, ("h", 0, 1))
                if n == IT:
                    pe.wait_ge(heads_a_emptied, b.count(QUADS + 1, 1))
                four_heads(heads_a, probs_a[:, n % A_BUFS, :, :], n, 0, lambda q, jt, h: v1[:, jt, h, :])

            def a_denominators(n):
                four_heads(heads_a, probs_a[:, n % A_BUFS, :, :], n, 1,
                           lambda q, jt, h: c1[:, jt, h, :]).then_inc(probs_a_used, 1)

            def a_step(ring, r, b, n):
                a_numerators(ring, r, b, n)
                a_denominators(n)

            def turn_back(ring, b, bank_of, numerators, denominators):
                ring.wait_free(pe, b, ("den",))
                for it in range(IT):
                    mm = nc.tensor.transpose(bank_of(("den",))[:, it * P:(it + 1) * P],
                                             denominators[:, it * P:(it + 1) * P], ident[:])
                mm.then_inc(ring.filled, 1)
                for n in range(2):
                    ring.wait_free(pe, b, ("back", n))
                    for t in range(2):
                        for q in range(QUADS):
                            it = 2 * n + t
                            mm = nc.tensor.transpose(as_rows(bank_of(("back", n)))[:, t, q * P:(q + 1) * P],
                                                     numerators[:, q, it * P:(it + 1) * P], ident[:])
                    mm.then_inc(ring.filled, 1)

            def a_back(b):
                pe.wait_ge(heads_a_emptied, b.count(QUADS + 1, QUADS + 1))
                turn_back(A, b, lambda key: bank_a(A, key), num_a, den_a)

            def second_layer(b, tiles=range(IT)):
                if 0 in tiles:
                    pe.wait_ge(probs_a_ready, b.count(A_PROBS, A_PROBS))
                    A.wait_emptied(pe, b, ("h", 1, 1))
                for it in tiles:
                    if it >= 2:
                        pe.wait_ge(rows2_emptied, b.count(IT, it - 1))
                    for jt in range(IT):
                        mm = nc.tensor.matmul(heads_a[:, it % 2, 0:D + 2],
                                              probs_a[:, NS % A_BUFS, jt, it * P:(it + 1) * P],
                                              v2[:, jt, :], start=(jt == 0), stop=(jt == IT - 1))
                    mm.then_inc(rows2_filled if it < IT - 1 else probs_a_used, 1)

            def turn_adjacency(b, tiles=range(IT)):
                pe.wait_ge(adj_loaded_again, b.count(16, 16))
                for jt in tiles:
                    A.wait_free(pe, b, ("adj_t", jt))
                    for it in range(IT):
                        mm = turn(bank_a(A, ("adj_t", jt)), adj_rows, jt, it)
                    mm.then_inc(A.filled, 1)

            def b_features(b):
                for m in range(KT):
                    Bb.wait_free(pe, b, ("feat", m))
                    for it in range(IT):
                        if m == 0:
                            pe.wait_ge(rows2_emptied, b.count(IT, it + 1))
                        mm = turn(bank_b(("feat", m)), x2, m, it)
                    mm.then_inc(Bb.filled, 1)

            def queries_or_keys(b, name, w):
                if name == "q":
                    for k in range(KT):
                        Bb.wait_emptied(pe, b, ("feat", k))
                for m in range(KT):
                    Bb.wait_free(pe, b, (name, m))
                    for k in range(KT):
                        mm = nc.tensor.matmul(bank_b((name, m)), w[:, k, m * P:(m + 1) * P],
                                              feat_b[:, k, :], start=(k == 0), stop=(k == KT - 1))
                    mm.then_inc(Bb.filled, 1)

            def gates(b):
                Bb.wait_free(pe, b, ("ac",))
                for k in range(KT):
                    mm = nc.tensor.matmul(bank_b(("ac",))[0:64, :], wg[:, k, :], feat_b[:, k, :],
                                          start=(k == 0), stop=(k == KT - 1))
                mm.then_inc(Bb.filled, 1)

            def values_3(b):
                for n in range(2):
                    rows_times(Bb, b, ("v", n), bank_b(("v", n)), feat_b, wv, n)

            def maxima(b, h, tiles=range(IT)):
                if h == 0 and 0 in tiles:
                    pe.wait_ge(gates_loaded, b.count(16 * 4, 16 * 4))
                if h < 4 and 0 in tiles:
                    pe.wait_ge(strip_loaded[h], b.count(16 * 6, 16 * 6))
                for it in tiles:
                    Bb.wait_free(pe, b, ("max", h, it))
                    nc.tensor.matmul(bank_b(("max", h, it)), q_stack[0:104, h, it * P:(it + 1) * P],
                                     k_stack[0:104, h, :], start=True, stop=True).then_inc(Bb.filled, 1)

            def turn_maxima(b, q):
                Bb.wait_emptied(pe, b, ("max", 4 * q + 3, IT - 1))
                Bb.wait_free(pe, b, ("max_t", q))
                for it in range(IT):
                    mm = nc.tensor.transpose(bank_b(("max_t", q))[0:4, it * P:(it + 1) * P],
                                             row_max[:, it, 4 * q:4 * q + 4], ident[:])
                mm.then_inc(Bb.filled, 1)

            def scores(b, n, heads=range(4)):
                q, jt = STEPS[n]
                if jt == 0 and 0 in heads:
                    pe.wait_ge(max_loaded, b.count(16 * QUADS, 16 * q + 16))
                for g in heads:
                    Bb.wait_free(pe, b, ("score", n, g))
                    nc.tensor.matmul(bank_b(("score", n, g)), k_stack[:, 4 * q + g, jt * P:(jt + 1) * P],
                                     q_stack[:, 4 * q + g, :], start=True, stop=True).then_inc(Bb.filled, 1)

            def b_numerators(b, n):
                if n == 0:
                    pe.wait_ge(heads_b_emptied, b.count(QUADS + 1))
                    Bb.wait_emptied(pe, b, ("v", 1))
                if n == IT:
                    pe.wait_ge(heads_b_emptied, b.count(QUADS + 1, 1))
                if n in DVE_STEPS:
                    pe.wait_ge(probs_b_vec, b.count(len(DVE_STEPS), DVE_STEPS.index(n) + 1))
                else:
                    pe.wait_ge(probs_b_pool, b.count(len(POOL_STEPS), POOL_STEPS.index(n) + 1))
                four_heads(heads_b, probs_b[:, n % B_BUFS, :, :], n, 0,
                           lambda q, jt, h: v3[:, jt, h * DH:(h + 1) * DH])

            def b_denominators(n):
                four_heads(heads_b, probs_b[:, n % B_BUFS, :, :], n, 1,
                           lambda q, jt, h: ones[:, q, :]).then_inc(probs_b_used, 1)

            def b_step(b, n):
                b_numerators(b, n)
                b_denominators(n)

            def b_back(b):
                pe.wait_ge(heads_b_emptied, b.count(QUADS + 1, QUADS + 1))
                turn_back(Bb, b, bank_b, num_b, den_b)

            def front(ring, r, n):
                a_features(ring, r, n, 0)
                source_and_target(ring, r, 0)
                turn_exp_adjacency(ring, r, n)
                factor_columns(ring, r, 0)
                for h in range(4):
                    g_everywhere(ring, r, n, h)
                values_1(ring, r)
                for h in range(4, H):
                    g_everywhere(ring, r, n, h)

            def first(a, n):
                front(A0, a, a)
                A0.wait_emptied(pe, a, ("g", H - 1))
                for s in range(NS):
                    a_step(A0, a, a, s)
                a_back(a)
                a_features(A, a, a, 1)
                source_and_target(A, a, 1)
                factor_columns(A, a, 1)
                g_everywhere_2(a)
                values_2(a)
                a_features(A, a, n, 0)
                source_and_target(A, a, 0)
                turn_exp_adjacency(A, a, n)
                second_layer(a)
                factor_columns(A, a, 0)
                for h in range(4):
                    g_everywhere(A, a, n, h)
                values_1(A, a)
                for h in range(4, H):
                    g_everywhere(A, a, n, h)
                for s in range(NS):
                    a_step(A, a, n, s)
                turn_adjacency(a)

            def pair(n, a, b):
                def num(s):
                    a_numerators(A, a, n, s)

                def g_pair(h):
                    g_everywhere(A, a, n, h)
                    g_everywhere(A, a, n, h + 1)

                a_back(a)
                b_features(b)
                queries_or_keys(b, "q", wq)
                gates(b)
                queries_or_keys(b, "k", wk)
                a_features(A, a, a, 1)
                source_and_target(A, a, 1)
                values_3(b)
                factor_columns(A, a, 1)
                g_everywhere_2(a)
                values_2(a)
                maxima(b, 0, (0, 1))
                a_features(A, a, n, 0)
                maxima(b, 0, (2, 3))
                second_layer(a, (0,))
                maxima(b, 1, (0, 1))
                source_and_target(A, a, 0)
                maxima(b, 1, (2, 3))
                second_layer(a, (1,))
                maxima(b, 2, (0, 1))
                second_layer(a, (2,))
                maxima(b, 2, (2, 3))
                turn_exp_adjacency(A, a, n)
                maxima(b, 3, (0, 1))
                second_layer(a, (3,))
                factor_columns(A, a, 0)
                maxima(b, 3, (2, 3))
                g_pair(0)
                turn_maxima(b, 0)
                g_pair(2)
                maxima(b, 4, (0, 1))
                values_1(A, a, (0,))
                maxima(b, 4, (2, 3))
                values_1(A, a, (1,))
                maxima(b, 5, (0, 1))
                g_pair(4)
                maxima(b, 5, (2, 3))
                g_pair(6)
                scores(b, 0)
                maxima(b, 6, (0, 1))
                num(0)
                maxima(b, 6, (2, 3))
                scores(b, 1, (0, 1))
                a_denominators(0)
                scores(b, 1, (2, 3))
                maxima(b, 7, (0, 1))
                num(1)
                maxima(b, 7, (2, 3))
                a_denominators(1)
                b_step(b, 0)
                turn_maxima(b, 1)
                num(2)
                scores(b, 2, (0, 1))
                a_denominators(2)
                scores(b, 2, (2, 3))
                b_numerators(b, 1)
                scores(b, 3, (0, 1))
                b_denominators(1)
                scores(b, 3, (2, 3))
                num(3)
                scores(b, 4, (0, 1))
                a_denominators(3)
                scores(b, 4, (2, 3))
                b_step(b, 2)
                scores(b, 5, (0, 1))
                num(4)
                scores(b, 5, (2, 3))
                a_denominators(4)
                b_step(b, 3)
                scores(b, 6, (0, 1))
                b_numerators(b, 4)
                scores(b, 6, (2, 3))
                b_denominators(4)
                scores(b, 7, (0, 1))
                num(5)
                scores(b, 7, (2, 3))
                a_denominators(5)
                b_step(b, 5)
                num(6)
                a_denominators(6)
                turn_adjacency(a, (0, 1))
                b_step(b, 6)
                turn_adjacency(a, (2, 3))
                b_step(b, 7)
                num(7)
                a_denominators(7)
                b_back(b)

            def last(b):
                b_features(b)
                queries_or_keys(b, "q", wq)
                gates(b)
                queries_or_keys(b, "k", wk)
                values_3(b)
                for h in range(4):
                    maxima(b, h)
                turn_maxima(b, 0)
                maxima(b, 4)
                maxima(b, 5)
                scores(b, 0)
                maxima(b, 6)
                scores(b, 1)
                maxima(b, 7)
                turn_maxima(b, 1)
                scores(b, 2)
                b_step(b, 0)
                for n in range(3, NS + 2):
                    if n < NS:
                        scores(b, n)
                    b_step(b, n - 2)
                b_back(b)

            loop(pe, first, pair, last)


_INS = ["x", "adj", "L0_gnn_W1", "L0_gnn_a_src1", "L0_gnn_a_dst1", "L0_gnn_g1", "L0_gnn_b1", "L0_gnn_W2",
        "L0_gnn_a_src2", "L0_gnn_a_dst2", "L0_gnn_g2", "L0_gnn_b2", "L1_gnn_W_q", "L1_gnn_b_q", "L1_gnn_W_k",
        "L1_gnn_b_k", "L1_gnn_W_v", "L1_gnn_b_v", "L1_gnn_w_g", "L1_gnn_b_g"]


def kernel(**inputs):
    import numpy as _np
    import concourse.bacc as _bacc
    from concourse import mybir as _mybir
    from concourse.bass_utils import run_bass_kernel_spmd as _run

    nc = _bacc.Bacc("TRN2", target_bir_lowering=False, num_devices=1)
    arrays, args = {}, []
    for name in _INS:
        a = _np.ascontiguousarray(inputs[name])
        if a.ndim == 0:
            a = a.reshape(1)
        arrays[f"in_{name}_dram"] = a
        args.append(nc.dram_tensor(f"in_{name}_dram", a.shape, _mybir.dt.from_np(a.dtype), kind="ExternalInput").ap())
    shape = inputs["x"].shape
    args.append(nc.dram_tensor("out_0_dram", shape, _mybir.dt.float32, kind="ExternalOutput").ap())
    two_gat_layers_then_biased_attention(nc, *args)
    r = _run(nc, [arrays], core_ids=[0])
    return r.results[0]["out_0_dram"]
```
